# Optimizing a Trainium2 kernel written in Bass

```python
import numpy as np
import jax
import jax.numpy as jnp

def _softmax(x, axis=-1):
    return jax.nn.softmax(x, axis=axis)

def _gelu(x):
    return jax.nn.gelu(x, approximate=True)

def _silu(x):
    return jax.nn.silu(x)

def _sigmoid(x):
    return jax.nn.sigmoid(x)

def _layernorm(x, axis=-1, eps=1e-05):
    m = jnp.mean(x, axis=axis, keepdims=True)
    v = jnp.var(x, axis=axis, keepdims=True)
    return (x - m) / jnp.sqrt(v + eps)

def _scatter_add(tgt, idx, src, axis=0):
    return tgt.at[idx].add(src)

def _segment_sum(src, seg, n):
    return jax.ops.segment_sum(src, seg, n)
kernel_name = 'mk_adj_preln_d1_adj_r2_2b2e38'

def setup_inputs(seed: int=0):
    np.random.seed(seed)
    _w = jnp.asarray

    def _rec_inputs():
        import jax
        import jax.numpy as jnp
        _gk = jax.random.key(seed)
        x = -0.0002928 + 1 * jax.random.normal(jax.random.fold_in(_gk, 1), (4096, 256), jnp.float32)
        _a = jax.random.bernoulli(jax.random.fold_in(_gk, 2), 0.00390625, (4096, 4096))
        adj = _a.astype(jnp.int32)
        return (x, adj)
    x, adj = _rec_inputs()

    def _L0_gnn_setup():
        import jax, jax.numpy as jnp
        import numpy as np
        N = 4096
        IN_F = 256
        OUT_F = 256
        ALPHA = 0.2
        key = jax.random.key(seed)
        k1, k2, k3, k4, k5 = jax.random.split(key, 5)
        inp = jax.random.normal(k1, (N, IN_F), dtype=jnp.float32)
        adj = jax.random.randint(k2, (N, N), 0, 2, dtype=jnp.int32)
        W1 = jax.random.normal(k3, (IN_F, OUT_F), dtype=jnp.float32) * (1.0 / np.sqrt(IN_F))
        b1 = jnp.zeros((OUT_F,), dtype=jnp.float32)
        a = jax.random.normal(k4, (2 * OUT_F,), dtype=jnp.float32) * (1.0 / np.sqrt(2 * OUT_F))
        a1 = a[:OUT_F]
        a2 = a[OUT_F:]
        b2 = jnp.zeros((), dtype=jnp.float32)
        return {'inp': inp, 'adj': adj, 'W1': W1, 'b1': b1, 'a1': a1, 'a2': a2, 'b2': b2}
    _L0_gnn_all = _L0_gnn_setup()
    _L0_gnn_in = {k: v for k, v in _L0_gnn_all.items() if k in ('W1', 'b1', 'a1', 'a2', 'b2')}
    del _L0_gnn_all
    return {'x': x, 'adj': adj, 'L0_gnn_W1': _L0_gnn_in['W1'], 'L0_gnn_b1': _L0_gnn_in['b1'], 'L0_gnn_a1': _L0_gnn_in['a1'], 'L0_gnn_a2': _L0_gnn_in['a2'], 'L0_gnn_b2': _L0_gnn_in['b2']}

def reference(x, adj, L0_gnn_W1, L0_gnn_b1, L0_gnn_a1, L0_gnn_a2, L0_gnn_b2):
    import jax
    import jax.numpy as jnp

    def _L0_gnn_ref(inp, adj, W1, b1, a1, a2, b2):
        import jax, jax.numpy as jnp
        import numpy as np
        N = 4096
        IN_F = 256
        OUT_F = 256
        ALPHA = 0.2
        h = inp @ W1 + b1
        e = jax.nn.leaky_relu((h @ a1)[:, None] + (h @ a2)[None, :] + b2, ALPHA)
        attention = jnp.where(adj > 0, e, jnp.float32(-1000000000000.0))
        attention = jax.nn.softmax(attention, axis=1)
        h_prime = attention @ h
        return jax.nn.elu(h_prime)
    h = jnp.maximum(_layernorm(x, axis=-1), 0.0)
    x = x + _L0_gnn_ref(h, adj, L0_gnn_W1, L0_gnn_b1, L0_gnn_a1, L0_gnn_a2, L0_gnn_b2)
    return x

_drawn_inputs = setup_inputs


def setup_inputs(seed=0):
    import zlib

    import numpy as np

    out = dict(_drawn_inputs(seed))
    spreads = {'L0_gnn_b1': (0.0, 0.1)}
    factors = {}
    for name, (base, spread) in spreads.items():
        noise = np.random.default_rng([zlib.crc32(name.encode()), seed]).standard_normal(out[name].shape)
        drawn = base * np.exp(spread * noise) if base else spread * noise
        out[name] = jnp.asarray(drawn.astype(out[name].dtype))
    for name, factor in factors.items():
        out[name] = (out[name] * factor).astype(out[name].dtype)
    return out
```

```python
from contextlib import ExitStack

import concourse.bass as bass
from concourse import mybir

P = 128
N = 4096
F = 256
KC = F // P
TILES = N // P
BANKS = 8
CW = BANKS * P
CHUNKS = N // CW
PAIRS = TILES // 2
SLOTS = 4
ROUNDS = PAIRS // SLOTS
GT = 4
GROUPS = TILES // GT
LOADS = 4
LT = TILES // LOADS
HW = F + 2
EPS = 1e-5
SLOPE = 0.2
TOP = 70.0
HALF = 4
FIRST_ROUND, LAST_ROUND = 0, ROUNDS - 1


def pair_no(ic, r, c):
    return ic * PAIRS + r * SLOTS + c


def source(r, c):
    return r * (2 * SLOTS) + 2 * c


def ahead(ic, r, c, k):
    if c + k < SLOTS:
        return ic, r, c + k
    if r is LAST_ROUND:
        return ic + 1, 0, c + k - SLOTS
    return ic, r + 1, c + k - SLOTS


def at_least(n, least):
    return not isinstance(n, int) or n >= least


def build(nc, adj_t, x, W1, b1, a1, a2, b2, out):
    fp32, fp32r, i32 = mybir.dt.float32, mybir.dt.float32r, mybir.dt.int32
    ALU, ACT, AX = mybir.AluOpType, mybir.ActivationFunctionType, mybir.AxisListType
    ds = bass.ds

    x_v = x.rearrange("(t p) f -> p t f", p=P)
    out_v = out.rearrange("(t p) f -> p t f", p=P)

    ctx = ExitStack()
    with ctx:
        def sb(name, shape, dt=fp32):
            return ctx.enter_context(nc.sbuf_tensor(name, shape, dt))

        def over(name, shape, dt, host, skip=0):
            return nc.alloc_sbuf_tensor_at(name, shape, dt, offset=nc.lookup_mloc(host).addr + skip)

        def sem(name):
            return ctx.enter_context(nc.semaphore(name))

        hp_hi = sb("hp_hi", [P, TILES, HW], fp32r)
        hp_lo = sb("hp_lo", [P, TILES, HW], fp32r)
        h_raw = over("h_raw", [P, TILES, HW], fp32, hp_lo)
        S = sb("S", [P, N])
        R = sb("R", [P, N])
        adj_s = sb("adj_s", [P, SLOTS, 2, CW], i32)
        adj_w = adj_s[:, :, :, :].bitcast(fp32)
        t_s = sb("t_s", [P, 2, 2, CW])
        w_hi = sb("w_hi", [P, 2, 2, CW], fp32r)
        w_lo = sb("w_lo", [P, 2, 2, CW], fp32r)
        y = sb("y", [P, BANKS, HW])
        r_s = sb("r_s", [P, HALF, F])
        e_s = sb("e_s", [P, HALF, F])
        o_s = sb("o_s", [P, HALF, F])
        x_lo = over("x_lo", [P, TILES // 2, F], fp32, w_hi)
        x_hi = over("x_hi", [P, TILES // 2, F], fp32, w_lo)
        x_half = [x_lo, x_hi]
        xn = over("xn", [P, 2, GT, F], fp32, t_s)
        hnT = over("hnT", [P, 2, KC, GT * P], fp32, t_s, 2 * GT * F * 4)
        junk = over("junk", [P, 6, F], fp32, y)

        W1x = sb("W1x", [P, KC, F + 1])
        a1rep = sb("a1rep", [P, KC, P])
        b1x = sb("b1x", [P, F + 1])
        ab = sb("ab", [P, 2, F])
        w1a1 = sb("w1a1", [P, KC])
        ident = sb("ident", [P, P])
        ones = sb("ones", [P, P])
        stats = sb("stats", [P, LT, 6])
        mom = sb("mom", [P, 4, LT])
        mean = sb("mean", [P, TILES])
        var = sb("var", [P, TILES])
        std = sb("std", [P, TILES])
        rstd = sb("rstd", [P, TILES])
        eps = sb("eps", [P, 1])
        ba = sb("ba", [P, 3])
        hs = sb("hs", [P, KC, GROUPS])
        hsum = sb("hsum", [P, KC])
        hsrep = sb("hsrep", [P, KC, P])
        h_mean = sb("h_mean", [P, F])
        gm = sb("gm", [P, 8])
        q = sb("q", [P, TILES])
        v = sb("v", [P, TILES])
        d8 = sb("d8", [P, TILES])
        flag = sb("flag", [P, BANKS])
        den = sb("den", [P, BANKS])
        rden = sb("rden", [P, BANKS])

        ps = ctx.enter_context(nc.psum_tensor("ps", [P, BANKS, 512], fp32))
        H0, S0 = 2, 6

        x_in = [sem(f"x_in{c}") for c in range(LOADS)]
        w_in = sem("w_in")
        vec_in = sem("vec_in")
        adj_in = [sem(f"adj_in{s}") for s in range(SLOTS)]
        pool_c = sem("pool_c")
        dve_c = sem("dve_c")
        const_ready = sem("const_ready")
        var_ready = sem("var_ready")
        std_ready = sem("std_ready")
        xn_ready = sem("xn_ready")
        tp_ready = sem("tp_ready")
        hn_ready = sem("hn_ready")
        h_ready = sem("h_ready")
        h_kept = sem("h_kept")
        s_ready = sem("s_ready")
        s_kept = sem("s_kept")
        hsrep_ready = sem("hsrep_ready")
        hmean_ps = sem("hmean_ps")
        hmean_kept = sem("hmean_kept")
        pmax_ready = sem("pmax_ready")
        pmaxT_ready = sem("pmaxT_ready")
        g1_ready = sem("g1_ready")
        g_ps = sem("g_ps")
        g_ready = sem("g_ready")
        qv_ready = sem("qv_ready")
        s2_used = sem("s2_used")
        S_ready = sem("S_ready")
        R_ready = sem("R_ready")
        ones_col = sem("ones_col")
        prep_done = sem("prep_done")
        eps_ready = sem("eps_ready")
        d8_ready = sem("d8_ready")
        hp_tile = sem("hp_tile")
        act_relu = sem("act_relu")
        dve_t = sem("dve_t")
        dve_y = sem("dve_y")
        hp_ready = sem("hp_ready")
        act_t = sem("act_t")
        masked = sem("masked")
        hi_ready = sem("hi_ready")
        lo_ready = sem("lo_ready")
        pe_done = sem("pe_done")
        bank_done = sem("bank_done")
        evacuated = sem("evacuated")
        y_ready = sem("y_ready")
        r_ready = sem("r_ready")
        e_ready = sem("e_ready")
        em_ready = sem("em_ready")
        xo_in = sem("xo_in")
        sum1 = sem("sum1")
        summed = sem("summed")
        used = sem("used")
        stored = sem("stored")

        block = ctx.enter_context(nc.Block())

        @block.sync
        def _(sp):
            for c in range(LOADS):
                half, off = x_half[c // 2], (c % 2) * LT
                sp.dma_start(half[:, off:off + LT, :], x_v[:, c * LT:(c + 1) * LT, :]).then_inc(x_in[c], 16)
            def load_adj(n, s):
                sp.dma_start(adj_s[:, s, :, :], adj_t[ds(n, 1), :, :, :].rearrange("a p s c -> p (a s) c"))\
                    .then_inc(adj_in[s], 16)

            def load_x(k):
                sp.dma_start(o_s[:, :, :], x_v[:, ds(k * HALF, HALF), :]).then_inc(xo_in, 16)

            def store(k):
                sp.wait_ge(summed, k + 1)
                sp.dma_start(out_v[:, ds(k * HALF, HALF), :], o_s[:, :, :]).then_inc(stored, 16)
                sp.wait_ge(stored, (k + 1) * 16)

            for s in range(SLOTS):
                load_adj(s, s)
            load_x(0)

            def chunk(ic, first=False, last=False):
                for r in range(ROUNDS):
                    for s in range(SLOTS):
                        n = pair_no(ic, r, s)
                        if not (last and r == LAST_ROUND):
                            sp.wait_ge(lo_ready, n + 1)
                            load_adj(n + SLOTS, s)
                        if not first and (r, s) == (2, 2):
                            store(2 * ic - 2)
                            load_x(2 * ic - 1)
                        if not first and (r, s) == (3, 3):
                            store(2 * ic - 1)
                            load_x(2 * ic)

            chunk(0, first=True)
            with sp.Fori(1, CHUNKS - 1) as ic:
                chunk(ic)
            chunk(CHUNKS - 1, last=True)
            store(2 * CHUNKS - 2)
            load_x(2 * CHUNKS - 1)
            store(2 * CHUNKS - 1)

        @block.gpsimd
        def _(pool):
            pool.memset(ones[:, :], 1.0).then_inc(pool_c, 1)
            pool.memset(ident[:, :], 0.0).then_inc(pool_c, 1)
            pool.wait_ge(pool_c, 2)
            pool.affine_select(out=ident[:, :], in_=ident[:, :], compare_op=ALU.not_equal, fill=1.0, base=0,
                               pattern=[[-1, P]], channel_multiplier=1).then_inc(pool_c, 1)
            pool.sem_inc(used, 1)
            with pool.Fori(0, 2 * CHUNKS) as k:
                pool.wait_ge(xo_in, (k + 1) * 16)
                pool.wait_ge(r_ready, k + 2)
                pool.tensor_tensor(o_s[:, :, :], o_s[:, :, :], r_s[:, :, :], ALU.add).then_inc(sum1, 1)
                pool.wait_ge(sum1, k + 1)
                pool.wait_ge(em_ready, k + 1)
                pool.tensor_tensor(o_s[:, :, :], o_s[:, :, :], e_s[:, :, :], ALU.add).then_inc(summed, 1)
                pool.wait_ge(summed, k + 1)
                pool.sem_inc(used, 1)

        @block.scalar
        def _(act):
            act.dma_start(W1x[:, :, 0:F], W1.rearrange("(c p) f -> p c f", p=P)).then_inc(w_in, 16)
            act.dma_start(ab[:, 0, :], a1.partition_broadcast(P)).then_inc(vec_in, 16)
            act.dma_start(ab[:, 1, :], a2.partition_broadcast(P)).then_inc(vec_in, 16)
            act.dma_start(b1x[:, 0:F], b1.partition_broadcast(P)).then_inc(vec_in, 16)
            act.dma_start(ba[:, 2:3], b2.partition_broadcast(P)).then_inc(vec_in, 16)

            def root(c):
                act.wait_ge(var_ready, c + 1)
                act.activation(std[:, c * LT:(c + 1) * LT], var[:, c * LT:(c + 1) * LT], ACT.Sqrt,
                               scale=1.0 / F, bias=eps[:, 0:1]).then_inc(std_ready, 1)

            def relu_T(g):
                u = g % 2
                if g >= 2:
                    act.wait_ge(s_ready, g - 1)
                for kc in range(KC):
                    act.wait_ge(tp_ready, KC * g + kc + 1)
                    act.activation(hnT[:, u, kc, :], ps[:, kc, :], ACT.Relu,
                                   accum_out=hs[:, kc, g:g + 1]).then_inc(hn_ready, 1)

            def keep_s(g):
                act.wait_ge(s_ready, g + 1)
                act.activation(S[:, g * GT * P:(g + 1) * GT * P], ps[:, S0 + g % 2, :], ACT.Copy).then_inc(s_kept, 1)

            act.wait_ge(eps_ready, 1)
            root(0)
            relu_T(0)
            for g in range(GROUPS):
                if g % 2 == 0 and g // 2 + 1 < LOADS:
                    root(g // 2 + 1)
                if g + 1 < GROUPS:
                    relu_T(g + 1)
                keep_s(g)

            act.wait_ge(g_ready, 1)
            act.activation(v[:, :], h_raw[:, :, F], ACT.Exp, scale=SLOPE, bias=gm[:, 5:6]).then_inc(qv_ready, 1)
            act.activation(q[:, :], h_raw[:, :, F], ACT.Exp, scale=1 - SLOPE, bias=gm[:, 4:5]).then_inc(qv_ready, 1)

            def exp_R(ic):
                act.activation(R[:, ds(ic * CW, CW)], S[:, ds(ic * CW, CW)], ACT.Exp).then_inc(R_ready, 1)

            def t_second(ic, r, c):
                n = pair_no(ic, r, c)
                buf = t_s[:, c % 2, 1, :]
                act.activation(buf, S[:, ds(ic * CW, CW)], ACT.Relu, bias=d8[:, ds(source(r, c) + 1, 1)])\
                    .then_inc(act_relu, 1)
                act.wait_ge(act_relu, n + 1)
                act.activation(buf, buf, ACT.Exp).then_inc(act_t, 1)

            def high(ic, r, c):
                n = pair_no(ic, r, c)
                act.wait_ge(masked, n + 1)
                if at_least(n, 2):
                    act.wait_ge(pe_done, n - 1)
                act.activation(w_hi[:, c % 2, :, :], adj_w[:, c, :, :], ACT.Copy).then_inc(hi_ready, 1)

            def hp_high(r, c):
                for s in range(2):
                    jb = source(r, c) + s
                    act.activation(hp_hi[:, ds(jb, 1), :], h_raw[:, ds(jb, 1), :], ACT.Copy,
                                   scale=v[:, ds(jb, 1)]).then_inc(hp_tile, 1)

            def evacuate(ic):
                if at_least(ic, 1):
                    act.wait_ge(r_ready, 2 * ic + 1)
                for ib in range(BANKS):
                    if ib < BANKS - 1:
                        act.wait_ge(bank_done, ic * (BANKS - 1) + ib + 1)
                    else:
                        act.wait_ge(pe_done, ic * PAIRS + PAIRS)
                    act.activation(y[:, ib, :], ps[:, ib, 0:HW], ACT.Copy).then_inc(evacuated, 1)

            def exp_y(ic, hf, js):
                for j in js:
                    ib = hf * HALF + j
                    act.activation(e_s[:, j, :].unsqueeze(1), y[:, ds(ib, 1), 0:F], ACT.Exp,
                                   scale=rden[:, ds(ib, 1)]).then_inc(e_ready, 1)

            def round_of(ic, r, first, last):
                for c in range(SLOTS):
                    if first and not (r is LAST_ROUND and c == SLOTS - 1):
                        hp_high(*ahead(ic, r, c, 1)[1:])
                    inner = r is not FIRST_ROUND and r is not LAST_ROUND
                    if r is FIRST_ROUND and c == 2 and not last:
                        act.wait_ge(S_ready, ic + 2)
                    if inner and c == 1 and not first:
                        act.wait_ge(y_ready, ic)
                        act.wait_ge(used, (ic - 1) * 2 + r)
                    high(ic, r, c)
                    if r is FIRST_ROUND and c == 0 and not first:
                        evacuate(ic - 1)
                    if not (last and r is LAST_ROUND and c >= SLOTS - 2):
                        t_second(*ahead(ic, r, c, 2))
                    if r is FIRST_ROUND and c == 2 and not last:
                        exp_R(ic + 1)
                    if inner and not first and c in (1, 2):
                        exp_y(ic - 1, r - 1, (2 * c - 2, 2 * c - 1))

            def chunk(ic, first=False, last=False):
                round_of(ic, FIRST_ROUND, first, last)
                with act.Fori(1, ROUNDS - 1) as r:
                    round_of(ic, r, first, last)
                round_of(ic, LAST_ROUND, first, last)

            act.wait_ge(S_ready, 1)
            exp_R(0)
            act.wait_ge(ones_col, 1)
            hp_high(0, 0)
            t_second(0, 0, 0)
            t_second(0, 0, 1)
            chunk(0, first=True)
            with act.Fori(1, CHUNKS - 1) as ic:
                chunk(ic)
            chunk(CHUNKS - 1, last=True)
            evacuate(CHUNKS - 1)
            act.wait_ge(y_ready, CHUNKS)
            for hf in range(2):
                act.wait_ge(used, (CHUNKS - 1) * 2 + hf + 1)
                exp_y(CHUNKS - 1, hf, range(HALF))

        @block.tensor
        def _(pe):
            def transposes(g, u):
                pe.wait_ge(xn_ready, g + 1)
                for kc in range(KC):
                    if at_least(g, 1):
                        pe.wait_ge(hn_ready, (g - 1) * KC + kc + 1)
                    for t in range(GT):
                        last = pe.transpose(ps[:, kc, t * P:(t + 1) * P], xn[:, u, t, kc * P:(kc + 1) * P],
                                            ident[:, :])
                    last.then_inc(tp_ready, 1)

            def project(g, u):
                pe.wait_ge(hn_ready, g * KC + KC)
                if at_least(g, 1):
                    pe.wait_ge(h_kept, g)
                for t in range(GT):
                    for kc in range(KC):
                        last = pe.matmul(ps[:, H0 + t, 0:F + 1], hnT[:, u, kc, t * P:(t + 1) * P], W1x[:, kc, :],
                                         start=kc == 0, stop=kc == KC - 1)
                last.then_inc(h_ready, 1)
                if at_least(g, 2):
                    pe.wait_ge(s_kept, g - 1)
                for kc in range(KC):
                    last = pe.matmul(ps[:, S0 + u, :], a1rep[:, kc, :], hnT[:, u, kc, :],
                                     start=kc == 0, stop=kc == KC - 1)
                last.then_inc(s_ready, 1)

            pe.wait_ge(pool_c, 3)
            transposes(0, 0)
            pe.wait_ge(const_ready, 1)
            transposes(1, 1)
            project(0, 0)
            transposes(2, 0)
            project(1, 1)
            with pe.Fori(1, GROUPS // 2 - 1) as k:
                transposes(2 * k + 1, 1)
                project(2 * k, 0)
                transposes(2 * k + 2, 0)
                project(2 * k + 1, 1)
            transposes(GROUPS - 1, 1)
            project(GROUPS - 2, 0)
            project(GROUPS - 1, 1)

            pe.wait_ge(hsrep_ready, 1)
            for kc in range(KC):
                last = pe.matmul(ps[:, 0, 0:F], hsrep[:, kc, :], W1x[:, kc, 0:F], start=kc == 0, stop=kc == KC - 1)
            last.then_inc(hmean_ps, 1)
            pe.wait_ge(pmax_ready, 1)
            pe.transpose(ps[0:1, 1, 0:P], gm[:, 0:1], ident[:, :]).then_inc(pmaxT_ready, 1)
            pe.wait_ge(g1_ready, 1)
            pe.matmul(ps[:, H0, 0:1], ones[0:1, 0:P], gm[0:1, 1:2], start=True, stop=True).then_inc(g_ps, 1)

            def pair(ic, m, b, first, start=False, stop=False):
                n = ic * PAIRS + m
                pe.wait_ge(lo_ready, n + 1)
                if first:
                    pe.wait_ge(hp_ready, 2 * m + 2)
                for s in range(2):
                    hh = hp_hi[:, ds(2 * m + s, 1), :]
                    hl = hp_lo[:, ds(2 * m + s, 1), :]
                    for ib in range(BANKS):
                        col = slice(ib * P, (ib + 1) * P)
                        acc = ps[:, ib, 0:HW].unsqueeze(1)
                        if start and s == 0 and not first:
                            pe.wait_ge(evacuated, ic * BANKS - BANKS + ib + 1)
                        pe.matmul(acc, w_hi[:, b, s, col], hh, start=start and s == 0, stop=False)
                        pe.matmul(acc, w_hi[:, b, s, col], hl, start=False, stop=False)
                        last = pe.matmul(acc, w_lo[:, b, s, col], hh, start=False, stop=stop and s == 1)
                        if stop and s == 1 and ib < BANKS - 1:
                            last.then_inc(bank_done, 1)
                last.then_inc(pe_done, 1)

            def chunk(ic, first=False):
                pair(ic, 0, 0, first, start=True)
                pair(ic, 1, 1, first)
                with pe.Fori(1, PAIRS // 2 - 1) as k:
                    pair(ic, 2 * k, 0, first)
                    pair(ic, 2 * k + 1, 1, first)
                pair(ic, PAIRS - 2, 0, first)
                pair(ic, PAIRS - 1, 1, first, stop=True)

            pe.wait_ge(prep_done, 1)
            chunk(0, first=True)
            with pe.Fori(1, CHUNKS) as ic:
                chunk(ic)

        @block.vector
        def _(dve):
            links = [0]

            def link(ins):
                links[0] += 1
                ins.then_inc(dve_c, 1)
                dve.wait_ge(dve_c, links[0])

            dve.sem_inc(r_ready, 1)
            dve.memset(eps[:, :], EPS).then_inc(eps_ready, 1)

            def moments(c):
                dve.wait_ge(x_in[c], 16)
                half, off = x_half[c // 2], (c % 2) * LT
                for t in range(LT):
                    last = dve.bn_stats(stats[:, t, :], half[:, off + t, :])
                link(last)
                dve.tensor_tensor(mom[:, 0, :], stats[:, :, 1], stats[:, :, 4], ALU.add)
                dve.tensor_tensor(mom[:, 1, :], stats[:, :, 1], stats[:, :, 4], ALU.subtract)
                link(dve.tensor_tensor(mom[:, 2, :], stats[:, :, 2], stats[:, :, 5], ALU.add))
                dve.tensor_scalar(mean[:, c * LT:(c + 1) * LT], mom[:, 0, :], 0.5, None, ALU.mult)
                link(dve.tensor_tensor(mom[:, 3, :], mom[:, 1, :], mom[:, 1, :], ALU.mult))
                dve.scalar_tensor_tensor(var[:, c * LT:(c + 1) * LT], mom[:, 3, :], F / 4.0, mom[:, 2, :],
                                         ALU.mult, ALU.add).then_inc(var_ready, 1)

            def inverse(c):
                dve.wait_ge(std_ready, c + 1)
                link(dve.reciprocal(rstd[:, c * LT:(c + 1) * LT], std[:, c * LT:(c + 1) * LT]))

            def normalise(g):
                if g >= 2:
                    dve.wait_ge(tp_ready, KC * (g - 1))
                half, off = x_half[g // (GROUPS // 2)], (g % (GROUPS // 2)) * GT
                for t in range(GT):
                    tile = g * GT + t
                    last = dve.tensor_scalar(xn[:, g % 2, t, :], half[:, off + t, :], mean[:, tile:tile + 1],
                                             rstd[:, tile:tile + 1], ALU.subtract, ALU.mult)
                last.then_inc(xn_ready, 1)

            def keep_h(g):
                dve.wait_ge(h_ready, g + 1)
                dve.tensor_tensor(h_raw[:, g * GT:(g + 1) * GT, 0:F + 1], ps[:, H0:H0 + GT, 0:F + 1],
                                  b1x[:, :].unsqueeze(1).broadcast_to([P, GT, F + 1]), ALU.add).then_inc(h_kept, 1)

            moments(0)
            inverse(0)
            normalise(0)
            normalise(1)
            dve.wait_ge(w_in, 16)
            dve.wait_ge(vec_in, 64)
            dve.memset(b1x[:, F:F + 1], 0.0)
            for kc in range(KC):
                for a, dst in ((0, w1a1[:, kc:kc + 1]), (1, W1x[:, kc, F:F + 1])):
                    dve.tensor_tensor_reduce(out=junk[:, 2 * kc + a, :], in0=W1x[:, kc, 0:F], in1=ab[:, a, :], scale=1.0, scalar=0.0,
                                             op0=ALU.mult, op1=ALU.add, accum_out=dst)
            dve.wait_ge(pool_c, 3)
            for a in range(2):
                last = dve.tensor_tensor_reduce(out=junk[:, 4 + a, :], in0=b1x[:, 0:F], in1=ab[:, a, :], scale=1.0, scalar=0.0,
                                                op0=ALU.mult, op1=ALU.add, accum_out=ba[:, a:a + 1])
            link(last)
            for kc in range(KC):
                last = dve.tensor_scalar(a1rep[:, kc, :], ones[:, :], w1a1[:, kc:kc + 1], 1 - SLOPE, ALU.mult, ALU.mult)
            last.then_inc(const_ready, 1)
            link(dve.tensor_tensor(gm[:, 6:7], ba[:, 0:1], ba[:, 1:2], ALU.add))
            link(dve.tensor_tensor(gm[:, 7:8], gm[:, 6:7], ba[:, 2:3], ALU.add))
            for c in range(LOADS):
                if c + 1 < LOADS:
                    moments(c + 1)
                    inverse(c + 1)
                    normalise(2 * c + 2)
                keep_h(2 * c)
                if c + 1 < LOADS:
                    normalise(2 * c + 3)
                keep_h(2 * c + 1)

            dve.wait_ge(h_kept, GROUPS)
            dve.reduce_max(gm[:, 0:1], h_raw[:, :, F], AX.X).then_inc(pmax_ready, 1)
            dve.wait_ge(hn_ready, GROUPS * KC)
            link(dve.reduce_sum(hsum[:, :], hs[:, :, :], AX.X))
            for kc in range(KC):
                last = dve.tensor_scalar(hsrep[:, kc, :], ones[:, :], hsum[:, kc:kc + 1], None, ALU.mult)
            last.then_inc(hsrep_ready, 1)
            dve.wait_ge(pmaxT_ready, 1)
            dve.reduce_max(gm[0:1, 1:2], ps[0:1, 1, 0:P], AX.X).then_inc(g1_ready, 1)
            dve.wait_ge(g_ps, 1)
            link(dve.tensor_copy(gm[:, 2:3], ps[:, H0, 0:1]))
            dve.tensor_scalar(gm[:, 4:5], gm[:, 2:3], -(1 - SLOPE), None, ALU.mult)
            dve.tensor_scalar(gm[:, 5:6], gm[:, 2:3], -SLOPE, None, ALU.mult)
            last = dve.tensor_scalar(gm[:, 3:4], gm[:, 2:3], gm[:, 7:8], 1 - SLOPE, ALU.add, ALU.mult)
            last.then_inc(g_ready, 1)
            dve.wait_ge(g_ready, 1)
            dve.tensor_scalar(d8[:, :], h_raw[:, :, F], 1 - SLOPE, gm[:, 4:5], ALU.mult, ALU.add).then_inc(d8_ready, 1)

            def finish_S(ic):
                part = S[:, ds(ic * CW, CW)]
                dve.tensor_scalar(part, part, gm[:, 3:4], TOP, ALU.add, ALU.min).then_inc(S_ready, 1)

            dve.wait_ge(s_kept, GROUPS)
            finish_S(0)
            dve.wait_ge(qv_ready, 2)
            dve.wait_ge(d8_ready, 1)
            dve.memset(h_raw[:, :, F], 1.0)
            dve.memset(h_raw[:, :, F + 1], 0.0).then_inc(ones_col, 1)
            dve.wait_ge(hmean_ps, 1)
            dve.scalar_tensor_tensor(h_mean[:, :], ps[:, 0, 0:F], 1.0 / N, b1x[:, 0:F], ALU.mult, ALU.add)\
                .then_inc(prep_done, 1)

            def hp_low(r, c):
                for s in range(2):
                    jb = source(r, c) + s
                    dve.wait_ge(hp_tile, jb + 1)
                    dve.scalar_tensor_tensor(hp_lo[:, ds(jb, 1), :], h_raw[:, ds(jb, 1), :], v[:, ds(jb, 1)],
                                             hp_hi[:, ds(jb, 1), :].bitcast(fp32), ALU.mult, ALU.subtract)\
                        .then_inc(hp_ready, 1)

            def t_first(ic, r, c):
                n = pair_no(ic, r, c)
                if at_least(n, 2):
                    dve.wait_ge(masked, n - 1)
                dve.tensor_scalar(t_s[:, c % 2, 0, :], R[:, ds(ic * CW, CW)], q[:, ds(source(r, c), 1)], 1.0,
                                  ALU.mult, ALU.max).then_inc(dve_t, 1)

            def mask(ic, r, c):
                n = pair_no(ic, r, c)
                dve.wait_ge(adj_in[c], (ic * ROUNDS + r + 1) * 16)
                dve.wait_ge(dve_t, n + 1)
                dve.wait_ge(act_t, n + 1)
                dve.scalar_tensor_tensor(adj_w[:, c, :, :], adj_s[:, c, :, :], 0.0, t_s[:, c % 2, :, :],
                                         ALU.is_gt, ALU.mult).then_inc(masked, 1)

            def low(ic, r, c):
                n = pair_no(ic, r, c)
                dve.wait_ge(hi_ready, n + 1)
                if at_least(n, 2):
                    dve.wait_ge(pe_done, n - 1)
                dve.tensor_tensor(w_lo[:, c % 2, :, :], adj_w[:, c, :, :], w_hi[:, c % 2, :, :].bitcast(fp32),
                                  ALU.subtract).then_inc(lo_ready, 1)

            def fix_y(ic):
                dve.wait_ge(evacuated, ic * BANKS + BANKS)
                dve.tensor_scalar(flag[:, :], y[:, :, F], 0.0, None, ALU.is_equal).then_inc(dve_y, 1)
                dve.wait_ge(dve_y, 3 * ic + 1)
                dve.tensor_tensor(den[:, :], y[:, :, F], flag[:, :], ALU.add).then_inc(dve_y, 1)
                dve.wait_ge(dve_y, 3 * ic + 2)
                dve.reciprocal(rden[:, :], den[:, :]).then_inc(dve_y, 1)
                dve.wait_ge(dve_y, 3 * ic + 3)
                for ib in range(BANKS):
                    last = dve.scalar_tensor_tensor(y[:, ib, 0:F], h_mean[:, :], flag[:, ib:ib + 1], y[:, ib, 0:F],
                                                    ALU.mult, ALU.add)
                last.then_inc(y_ready, 1)

            def relu_y(ic, hf):
                dve.wait_ge(y_ready, ic + 1)
                dve.wait_ge(used, ic * 2 + hf + 1)
                for j in range(HALF):
                    ib = hf * HALF + j
                    last = dve.tensor_scalar(r_s[:, j, :].unsqueeze(1), y[:, ds(ib, 1), 0:F], rden[:, ds(ib, 1)], 0.0,
                                             ALU.mult, ALU.max)
                last.then_inc(r_ready, 1)

            def expm1_y(ic, hf):
                dve.wait_ge(e_ready, (ic * 2 + hf + 1) * HALF)
                dve.tensor_scalar(e_s[:, :, :], e_s[:, :, :], 1.0, -1.0, ALU.min, ALU.add).then_inc(em_ready, 1)

            def round_of(ic, r, first, last):
                inner = r is not FIRST_ROUND and r is not LAST_ROUND
                for c in range(SLOTS):
                    end = last and r is LAST_ROUND
                    if first and not (r is LAST_ROUND and c == SLOTS - 1):
                        hp_low(*ahead(ic, r, c, 1)[1:])
                    if not (end and c == SLOTS - 1):
                        mask(*ahead(ic, r, c, 1))
                    if not (end and c >= SLOTS - 2):
                        t_first(*ahead(ic, r, c, 2))
                    low(ic, r, c)
                    if r is FIRST_ROUND and c == 1 and not last:
                        finish_S(ic + 1)
                    if r is FIRST_ROUND and c == 2 and not first:
                        fix_y(ic - 1)
                    if inner and c == 1 and not first:
                        relu_y(ic - 1, r - 1)
                    if inner and c == 3 and not first:
                        expm1_y(ic - 1, r - 1)
                    if r is LAST_ROUND and c == 0 and not last:
                        dve.wait_ge(R_ready, ic + 2)

            def chunk(ic, first=False, last=False):
                round_of(ic, FIRST_ROUND, first, last)
                with dve.Fori(1, ROUNDS - 1) as r:
                    round_of(ic, r, first, last)
                round_of(ic, LAST_ROUND, first, last)

            dve.wait_ge(R_ready, 1)
            t_first(0, 0, 0)
            t_first(0, 0, 1)
            hp_low(0, 0)
            mask(0, 0, 0)
            chunk(0, first=True)
            with dve.Fori(1, CHUNKS - 1) as ic:
                chunk(ic)
            chunk(CHUNKS - 1, last=True)
            fix_y(CHUNKS - 1)
            for hf in range(2):
                relu_y(CHUNKS - 1, hf)
                expm1_y(CHUNKS - 1, hf)


def kernel(x, adj, L0_gnn_W1, L0_gnn_b1, L0_gnn_a1, L0_gnn_a2, L0_gnn_b2):
    import numpy as np
    import concourse.bacc as bacc
    from concourse.bass_utils import run_bass_kernel_spmd

    tiles = np.asarray(adj).reshape(CHUNKS, CW, PAIRS, 2, P).transpose(0, 2, 4, 3, 1)
    arrays = {
        "adj_t": np.ascontiguousarray(tiles.reshape(CHUNKS * PAIRS, P, 2, CW)),
        "x": np.ascontiguousarray(x),
        "W1": np.ascontiguousarray(L0_gnn_W1),
        "b1": np.ascontiguousarray(L0_gnn_b1),
        "a1": np.ascontiguousarray(L0_gnn_a1),
        "a2": np.ascontiguousarray(L0_gnn_a2),
        "b2": np.ascontiguousarray(L0_gnn_b2).reshape(1),
    }
    nc = bacc.Bacc("TRN2", target_bir_lowering=False, num_devices=1)
    args = [nc.dram_tensor(name, a.shape, mybir.dt.from_np(a.dtype), kind="ExternalInput").ap()
            for name, a in arrays.items()]
    out = nc.dram_tensor("out", (N, F), mybir.dt.float32, kind="ExternalOutput").ap()
    build(nc, *args, out)
    r = run_bass_kernel_spmd(nc, [arrays], core_ids=[0])
    return r.results[0]["out"]
```

```python
from contextlib import ExitStack

import concourse.bass as bass
from concourse import mybir

P = 128
N = 4096
F = 256
KC = F // P
TILES = N // P
BANKS = 8
CW = BANKS * P
CHUNKS = N // CW
PAIRS = TILES // 2
SLOTS = 4
ROUNDS = PAIRS // SLOTS
GT = 4
GROUPS = TILES // GT
HW = F + 2
EPS = 1e-5
SLOPE = 0.2
TOP = 70.0
HALF = 4
TINY = 2.0 ** -100
BOTH = (1,)
FIRST_ROUND, LAST_ROUND = 0, ROUNDS - 1


def pair_no(ic, r, c):
    return ic * PAIRS + r * SLOTS + c


def source(r, c):
    return r * (2 * SLOTS) + 2 * c


def ahead(ic, r, c, k):
    if c + k < SLOTS:
        return ic, r, c + k
    if r is LAST_ROUND:
        return ic + 1, 0, c + k - SLOTS
    return ic, r + 1, c + k - SLOTS


def vector_t(ic, r, c):
    mine = [k for k in range(SLOTS) if k not in BOTH]
    return (ic * ROUNDS + r) * len(mine) + sum(k <= c for k in mine)


def at_least(n, least):
    return not isinstance(n, int) or n >= least


def build(nc, adj_t, x, W1, b1, a1, a2, b2, out):
    fp32, fp32r, i32 = mybir.dt.float32, mybir.dt.float32r, mybir.dt.int32
    ALU, ACT, AX = mybir.AluOpType, mybir.ActivationFunctionType, mybir.AxisListType
    ds = bass.ds

    x_v = x.rearrange("(t p) f -> p t f", p=P)
    out_v = out.rearrange("(t p) f -> p t f", p=P)

    ctx = ExitStack()
    with ctx:
        def sb(name, shape, dt=fp32):
            return ctx.enter_context(nc.sbuf_tensor(name, shape, dt))

        def over(name, shape, dt, host, skip=0):
            return nc.alloc_sbuf_tensor_at(name, shape, dt, offset=nc.lookup_mloc(host).addr + skip)

        def sem(name):
            return ctx.enter_context(nc.semaphore(name))

        hp_hi = sb("hp_hi", [P, TILES, HW], fp32r)
        hp_lo = sb("hp_lo", [P, TILES, HW], fp32r)
        h_raw = over("h_raw", [P, TILES, HW], fp32, hp_lo)
        S = sb("S", [P, N])
        R = sb("R", [P, N])
        adj_s = sb("adj_s", [P, SLOTS, 2, CW], i32)
        adj_w = adj_s[:, :, :, :].bitcast(fp32)
        t_s = sb("t_s", [P, 2, 2, CW])
        w_hi = sb("w_hi", [P, 2, 2, CW], fp32r)
        w_lo = sb("w_lo", [P, 2, 2, CW], fp32r)
        y = sb("y", [P, BANKS, HW])
        e_s = sb("e_s", [P, HALF, F])
        o_s = sb("o_s", [P, BANKS, F])
        x_lo = over("x_lo", [P, TILES // 2, F], fp32, w_hi)
        x_hi = over("x_hi", [P, TILES // 2, F], fp32, w_lo)
        x_half = [x_lo, x_hi]
        xn = over("xn", [P, 2, GT, F], fp32, t_s)
        hnT = over("hnT", [P, 2, KC, GT * P], fp32, t_s, 2 * GT * F * 4)
        junk = over("junk", [P, 6, F], fp32, y)
        s1rep = over("s1rep", [P, 2, GT, P], fp32, e_s)
        hsrep = over("hsrep", [P, KC, P], fp32, o_s)
        x_end = adj_w[:, 0, :, :].rearrange("p s (b f) -> p (s b) f", f=F)
        e_end = t_s[:, 0, :, :].rearrange("p s (b f) -> p (s b) f", f=F)

        W1x = sb("W1x", [P, KC, HW])
        b1x = sb("b1x", [P, HW])
        ab = sb("ab", [P, 2, F])
        w1a1 = sb("w1a1", [P, KC])
        ident = sb("ident", [P, P])
        ones = sb("ones", [P, P])
        stats = sb("stats", [P, GROUPS, GT, 6])
        mom = sb("mom", [P, GROUPS, 4, GT])
        mean = sb("mean", [P, TILES])
        var = sb("var", [P, TILES])
        std = sb("std", [P, TILES])
        rstd = sb("rstd", [P, TILES])
        eps = sb("eps", [P, 1])
        ba = sb("ba", [P, 3])
        hs = sb("hs", [P, KC, GROUPS])
        hsum = sb("hsum", [P, KC])
        h_sum = sb("h_sum", [P, HW])
        h_tiny = sb("h_tiny", [P, HW], fp32r)
        ones64 = sb("ones64", [P, P], fp32r)
        gm = sb("gm", [P, 8])
        q = sb("q", [P, TILES])
        v = sb("v", [P, TILES])
        d8 = sb("d8", [P, TILES])
        rden = sb("rden", [P, BANKS])

        ps = ctx.enter_context(nc.psum_tensor("ps", [P, BANKS, 512], fp32))
        H0, S0 = 2, 6

        x_in = [sem(f"x_in{g}") for g in range(GROUPS)]
        w_in = sem("w_in")
        vec_in = sem("vec_in")
        adj_in = [sem(f"adj_in{s}") for s in range(SLOTS)]
        pool_c = sem("pool_c")
        dve_c = sem("dve_c")
        const_ready = sem("const_ready")
        s1_ready = sem("s1_ready")
        var_ready = sem("var_ready")
        std_ready = sem("std_ready")
        xn_ready = sem("xn_ready")
        tp_ready = sem("tp_ready")
        hn_ready = sem("hn_ready")
        h_ready = sem("h_ready")
        h_kept = sem("h_kept")
        s_ready = sem("s_ready")
        s_kept = sem("s_kept")
        hsrep_ready = sem("hsrep_ready")
        hsum_ps = sem("hsum_ps")
        pmax_ready = sem("pmax_ready")
        pmaxT_ready = sem("pmaxT_ready")
        g1_ready = sem("g1_ready")
        g_ps = sem("g_ps")
        g_ready = sem("g_ready")
        qv_ready = sem("qv_ready")
        s2_used = sem("s2_used")
        S_ready = sem("S_ready")
        R_ready = sem("R_ready")
        ones_col = sem("ones_col")
        prep_done = sem("prep_done")
        eps_ready = sem("eps_ready")
        d8_ready = sem("d8_ready")
        hp_tile = sem("hp_tile")
        act_relu = sem("act_relu")
        dve_t = sem("dve_t")
        dve_y = sem("dve_y")
        dve_o = sem("dve_o")
        hp_ready = sem("hp_ready")
        act_t = sem("act_t")
        masked = sem("masked")
        hi_ready = sem("hi_ready")
        lo_ready = sem("lo_ready")
        pe_done = sem("pe_done")
        bank_done = sem("bank_done")
        evacuated = sem("evacuated")
        y_ready = sem("y_ready")
        e_ready = sem("e_ready")
        xo_in = sem("xo_in")
        x_end_in = sem("x_end_in")
        summed = sem("summed")
        rd_end = sem("rd_end")
        e_end_ready = sem("e_end_ready")
        em_end = sem("em_end")
        elu_end = sem("elu_end")
        o_end = sem("o_end")
        stored = sem("stored")
        stored_end = sem("stored_end")

        block = ctx.enter_context(nc.Block())

        @block.sync
        def _(sp):
            for g in range(GROUPS):
                half, off = x_half[g // (GROUPS // 2)], (g % (GROUPS // 2)) * GT
                sp.dma_start(half[:, off:off + GT, :], x_v[:, g * GT:(g + 1) * GT, :]).then_inc(x_in[g], 16)

            def load_adj(n, s):
                sp.dma_start(adj_s[:, s, :, :], adj_t[ds(n, 1), :, :, :].rearrange("a p s c -> p (a s) c"))\
                    .then_inc(adj_in[s], 16)

            def load_x(ic):
                sp.dma_start(o_s[:, :, :], x_v[:, ds(ic * BANKS, BANKS), :]).then_inc(xo_in, 16)

            def store(ic, hf):
                sp.wait_ge(summed, ic * 2 + hf + 2)
                sp.dma_start(out_v[:, ds(ic * BANKS + hf * HALF, HALF), :], o_s[:, hf * HALF:(hf + 1) * HALF, :])\
                    .then_inc(stored, 16)

            for s in range(SLOTS):
                load_adj(s, s)

            def chunk(ic, first=False, last=False):
                for r in range(ROUNDS):
                    for s in range(SLOTS):
                        n = pair_no(ic, r, s)
                        if not (last and r == LAST_ROUND):
                            sp.wait_ge(lo_ready, n + 1)
                            load_adj(n + SLOTS, s)
                        if not first and r in (2, 3) and s == 0:
                            store(ic - 1, r - 2)
                        if not last and (r, s) == (3, 3):
                            if not first:
                                sp.wait_ge(stored, ic * 32)
                            load_x(ic)
                        if last and (r, s) == (3, 0):
                            sp.wait_ge(lo_ready, n + 1)
                            sp.dma_start(x_end, x_v[:, (CHUNKS - 1) * BANKS:CHUNKS * BANKS, :]).then_inc(x_end_in, 16)

            chunk(0, first=True)
            with sp.Fori(1, CHUNKS - 1) as ic:
                chunk(ic)
            chunk(CHUNKS - 1, last=True)
            for ib in range(BANKS):
                sp.wait_ge(o_end, ib + 1)
                sp.dma_start(out_v[:, (CHUNKS - 1) * BANKS + ib, :], x_end[:, ib, :]).then_inc(stored_end, 16)
            sp.wait_ge(stored, (CHUNKS - 1) * 32)
            sp.wait_ge(stored_end, BANKS * 16)

        @block.gpsimd
        def _(pool):
            pool.memset(ones[:, :], 1.0).then_inc(pool_c, 1)
            pool.memset(ident[:, :], 0.0).then_inc(pool_c, 1)
            pool.wait_ge(pool_c, 2)
            pool.affine_select(out=ident[:, :], in_=ident[:, :], compare_op=ALU.not_equal, fill=1.0, base=0,
                               pattern=[[-1, P]], channel_multiplier=1).then_inc(pool_c, 1)

        @block.scalar
        def _(act):
            act.dma_start(W1x[:, :, 0:F], W1.rearrange("(c p) f -> p c f", p=P)).then_inc(w_in, 16)
            act.dma_start(ab[:, 0, :], a1.partition_broadcast(P)).then_inc(vec_in, 16)
            act.dma_start(ab[:, 1, :], a2.partition_broadcast(P)).then_inc(vec_in, 16)
            act.dma_start(b1x[:, 0:F], b1.partition_broadcast(P)).then_inc(vec_in, 16)
            act.dma_start(ba[:, 2:3], b2.partition_broadcast(P)).then_inc(vec_in, 16)

            def root(g):
                act.wait_ge(var_ready, g + 1)
                act.activation(std[:, g * GT:(g + 1) * GT], var[:, g * GT:(g + 1) * GT], ACT.Sqrt,
                               scale=1.0 / F, bias=eps[:, 0:1]).then_inc(std_ready, 1)

            def relu_T(g):
                if g >= 2:
                    act.wait_ge(h_ready, g - 1)
                for kc in range(KC):
                    act.wait_ge(tp_ready, KC * g + kc + 1)
                    act.activation(hnT[:, g % 2, kc, :], ps[:, kc, :], ACT.Relu,
                                   accum_out=hs[:, kc, g:g + 1]).then_inc(hn_ready, 1)

            def repeat_s1(g):
                if g >= 2:
                    act.wait_ge(s_ready, g - 1)
                act.wait_ge(h_kept, g + 1)
                act.activation(s1rep[:, g % 2, :, :],
                               h_raw[:, g * GT:(g + 1) * GT, F + 1:F + 2].broadcast_to([P, GT, P]),
                               ACT.Copy).then_inc(s1_ready, 1)

            def keep_s(g):
                act.wait_ge(s_ready, g + 1)
                act.activation(S[:, g * GT * P:(g + 1) * GT * P], ps[:, S0 + g % 2, :], ACT.Copy).then_inc(s_kept, 1)

            act.wait_ge(eps_ready, 1)
            root(0)
            root(1)
            relu_T(0)
            for g in range(GROUPS):
                if g + 2 < GROUPS:
                    root(g + 2)
                if g + 1 < GROUPS:
                    relu_T(g + 1)
                repeat_s1(g)
                if g >= 1:
                    keep_s(g - 1)
            keep_s(GROUPS - 1)

            act.wait_ge(g_ready, 1)
            act.activation(v[:, :], h_raw[:, :, F], ACT.Exp, scale=SLOPE, bias=gm[:, 5:6]).then_inc(qv_ready, 1)
            act.activation(q[:, :], h_raw[:, :, F], ACT.Exp, scale=1 - SLOPE, bias=gm[:, 4:5]).then_inc(qv_ready, 1)

            def exp_R(ic):
                act.activation(R[:, ds(ic * CW, CW)], S[:, ds(ic * CW, CW)], ACT.Exp).then_inc(R_ready, 1)

            def t_part(ic, r, c):
                n = pair_no(ic, r, c)
                mine = (0, 1) if c in BOTH else (1,)
                for s in mine:
                    last = act.activation(t_s[:, c % 2, s, :], S[:, ds(ic * CW, CW)], ACT.Relu,
                                          bias=d8[:, ds(source(r, c) + s, 1)])
                last.then_inc(act_relu, 1)
                act.wait_ge(act_relu, n + 1)
                buf = t_s[:, c % 2, mine[0]:2, :]
                act.activation(buf, buf, ACT.Exp).then_inc(act_t, 1)

            def high(ic, r, c):
                n = pair_no(ic, r, c)
                act.wait_ge(masked, n + 1)
                if at_least(n, 2):
                    act.wait_ge(pe_done, n - 1)
                act.activation(w_hi[:, c % 2, :, :], adj_w[:, c, :, :], ACT.Copy).then_inc(hi_ready, 1)

            def hp_high(r, c):
                for s in range(2):
                    jb = source(r, c) + s
                    act.activation(hp_hi[:, ds(jb, 1), :], h_raw[:, ds(jb, 1), :], ACT.Copy,
                                   scale=v[:, ds(jb, 1)]).then_inc(hp_tile, 1)

            def evacuate(ic):
                act.wait_ge(summed, 2 * ic + 1)
                for ib in range(BANKS):
                    if ib < BANKS - 1:
                        act.wait_ge(bank_done, ic * (BANKS - 1) + ib + 1)
                    else:
                        act.wait_ge(pe_done, ic * PAIRS + PAIRS)
                    act.activation(y[:, ib, :], ps[:, ib, 0:HW], ACT.Copy).then_inc(evacuated, 1)

            def exp_y(ic, hf, js):
                for j in js:
                    ib = hf * HALF + j
                    act.activation(e_s[:, j, :].unsqueeze(1), y[:, ds(ib, 1), 0:F], ACT.Exp,
                                   scale=rden[:, ds(ib, 1)]).then_inc(e_ready, 1)

            def round_of(ic, r, first, last):
                for c in range(SLOTS):
                    if first and not (r is LAST_ROUND and c == SLOTS - 1):
                        hp_high(*ahead(ic, r, c, 1)[1:])
                    inner = r is not FIRST_ROUND and r is not LAST_ROUND
                    if r is FIRST_ROUND and c == 2 and not last:
                        act.wait_ge(S_ready, ic + 2)
                    if inner and c == 1 and not first:
                        act.wait_ge(y_ready, ic)
                        act.wait_ge(summed, (ic - 1) * 2 + r)
                    high(ic, r, c)
                    if r is FIRST_ROUND and c == 0 and not first:
                        evacuate(ic - 1)
                    if not (last and r is LAST_ROUND and c >= SLOTS - 2):
                        t_part(*ahead(ic, r, c, 2))
                    if r is FIRST_ROUND and c == 2 and not last:
                        exp_R(ic + 1)
                    if inner and not first and c in (1, 2):
                        exp_y(ic - 1, r - 1, (2 * c - 2, 2 * c - 1))

            def chunk(ic, first=False, last=False):
                round_of(ic, FIRST_ROUND, first, last)
                with act.Fori(1, ROUNDS - 1) as r:
                    round_of(ic, r, first, last)
                round_of(ic, LAST_ROUND, first, last)

            act.wait_ge(S_ready, 1)
            exp_R(0)
            act.wait_ge(ones_col, 1)
            hp_high(0, 0)
            t_part(0, 0, 0)
            t_part(0, 0, 1)
            chunk(0, first=True)
            with act.Fori(1, CHUNKS - 1) as ic:
                chunk(ic)
            chunk(CHUNKS - 1, last=True)
            for ib in range(BANKS):
                act.wait_ge(rd_end, ib + 1)
                act.activation(e_end[:, ib, :], ps[:, ib, 0:F], ACT.Exp, scale=rden[:, ib:ib + 1]).then_inc(e_end_ready, 1)

        @block.tensor
        def _(pe):
            def transposes(g, u):
                pe.wait_ge(xn_ready, g + 1)
                for kc in range(KC):
                    if at_least(g, 1):
                        pe.wait_ge(hn_ready, (g - 1) * KC + kc + 1)
                    for t in range(GT):
                        last = pe.transpose(ps[:, kc, t * P:(t + 1) * P], xn[:, u, t, kc * P:(kc + 1) * P],
                                            ident[:, :])
                    last.then_inc(tp_ready, 1)

            def project(g, u):
                pe.wait_ge(hn_ready, g * KC + KC)
                if at_least(g, 1):
                    pe.wait_ge(h_kept, g)
                for t in range(GT):
                    for kc in range(KC):
                        last = pe.matmul(ps[:, H0 + t, 0:HW], hnT[:, u, kc, t * P:(t + 1) * P], W1x[:, kc, :],
                                         start=kc == 0, stop=kc == KC - 1)
                last.then_inc(h_ready, 1)

            def spread(g, u):
                pe.wait_ge(s1_ready, g + 1)
                if at_least(g, 2):
                    pe.wait_ge(s_kept, g - 1)
                for t in range(GT):
                    last = pe.transpose(ps[:, S0 + u, t * P:(t + 1) * P], s1rep[:, u, t, :], ident[:, :])
                last.then_inc(s_ready, 1)

            pe.wait_ge(pool_c, 3)
            transposes(0, 0)
            pe.wait_ge(const_ready, 1)
            transposes(1, 1)
            project(0, 0)
            transposes(2, 0)
            project(1, 1)
            spread(0, 0)
            transposes(3, 1)
            project(2, 0)
            spread(1, 1)
            with pe.Fori(2, GROUPS // 2) as k:
                transposes(2 * k, 0)
                project(2 * k - 1, 1)
                spread(2 * k - 2, 0)
                transposes(2 * k + 1, 1)
                project(2 * k, 0)
                spread(2 * k - 1, 1)
            project(GROUPS - 1, 1)
            spread(GROUPS - 2, 0)
            spread(GROUPS - 1, 1)

            pe.wait_ge(hsrep_ready, 1)
            for kc in range(KC):
                last = pe.matmul(ps[:, 0, 0:F], hsrep[:, kc, :], W1x[:, kc, 0:F], start=kc == 0, stop=kc == KC - 1)
            last.then_inc(hsum_ps, 1)
            pe.wait_ge(pmax_ready, 1)
            pe.transpose(ps[0:1, 1, 0:P], gm[:, 0:1], ident[:, :]).then_inc(pmaxT_ready, 1)
            pe.wait_ge(g1_ready, 1)
            pe.matmul(ps[:, H0, 0:1], ones[0:1, 0:P], gm[0:1, 1:2], start=True, stop=True).then_inc(g_ps, 1)

            def begin(ic, first):
                for ib in range(BANKS):
                    if not first:
                        pe.wait_ge(evacuated, (ic - 1) * BANKS + ib + 1)
                    pe.matmul(ps[:, ib, 0:HW], ones64[:, :], h_tiny[:, :], start=True, stop=False)

            def pair(ic, m, b, first):
                n = ic * PAIRS + m
                if first:
                    pe.wait_ge(hp_ready, 2 * m + 2)
                for part, w in ((0, w_hi), (1, w_lo)):
                    pe.wait_ge((hi_ready, lo_ready)[part], n + 1)
                    for s in range(2):
                        hh = hp_hi[:, ds(2 * m + s, 1), :]
                        hl = hp_lo[:, ds(2 * m + s, 1), :]
                        for ib in range(BANKS):
                            acc = ps[:, ib, 0:HW].unsqueeze(1)
                            block_w = w[:, b, s, ib * P:(ib + 1) * P]
                            last = pe.matmul(acc, block_w, hh, start=False, stop=False)
                            if part == 0:
                                pe.matmul(acc, block_w, hl, start=False, stop=False)
                last.then_inc(pe_done, 1)

            def last_pair(ic, m, b, first):
                pe.wait_ge(lo_ready, ic * PAIRS + m + 1)
                if first:
                    pe.wait_ge(hp_ready, 2 * m + 2)
                for ib in range(BANKS):
                    acc = ps[:, ib, 0:HW].unsqueeze(1)
                    col = slice(ib * P, (ib + 1) * P)
                    for s in range(2):
                        hh = hp_hi[:, ds(2 * m + s, 1), :]
                        hl = hp_lo[:, ds(2 * m + s, 1), :]
                        pe.matmul(acc, w_hi[:, b, s, col], hh, start=False, stop=False)
                        pe.matmul(acc, w_hi[:, b, s, col], hl, start=False, stop=False)
                        last = pe.matmul(acc, w_lo[:, b, s, col], hh, start=False, stop=s == 1)
                    if ib < BANKS - 1:
                        last.then_inc(bank_done, 1)
                last.then_inc(pe_done, 1)

            def chunk(ic, first=False):
                begin(ic, first)
                with pe.Fori(0, PAIRS // 2 - 1) as k:
                    pair(ic, 2 * k, 0, first)
                    pair(ic, 2 * k + 1, 1, first)
                pair(ic, PAIRS - 2, 0, first)
                last_pair(ic, PAIRS - 1, 1, first)

            pe.wait_ge(prep_done, 1)
            chunk(0, first=True)
            with pe.Fori(1, CHUNKS) as ic:
                chunk(ic)

        @block.vector
        def _(dve):
            links = [0]

            def link(ins):
                links[0] += 1
                ins.then_inc(dve_c, 1)
                dve.wait_ge(dve_c, links[0])

            dve.sem_inc(summed, 1)
            dve.memset(eps[:, :], EPS).then_inc(eps_ready, 1)

            def moments(g):
                dve.wait_ge(x_in[g], 16)
                half, off = x_half[g // (GROUPS // 2)], (g % (GROUPS // 2)) * GT
                st, mo = stats[:, g, :, :], mom[:, g, :, :]
                for t in range(GT):
                    last = dve.bn_stats(st[:, t, :], half[:, off + t, :])
                link(last)
                dve.tensor_tensor(mo[:, 0, :], st[:, :, 1], st[:, :, 4], ALU.add)
                dve.tensor_tensor(mo[:, 1, :], st[:, :, 1], st[:, :, 4], ALU.subtract)
                link(dve.tensor_tensor(mo[:, 2, :], st[:, :, 2], st[:, :, 5], ALU.add))
                dve.tensor_scalar(mean[:, g * GT:(g + 1) * GT], mo[:, 0, :], 0.5, None, ALU.mult)
                link(dve.tensor_tensor(mo[:, 3, :], mo[:, 1, :], mo[:, 1, :], ALU.mult))
                dve.scalar_tensor_tensor(var[:, g * GT:(g + 1) * GT], mo[:, 3, :], F / 4.0, mo[:, 2, :],
                                         ALU.mult, ALU.add).then_inc(var_ready, 1)

            def normalise(g):
                dve.wait_ge(std_ready, g + 1)
                link(dve.reciprocal(rstd[:, g * GT:(g + 1) * GT], std[:, g * GT:(g + 1) * GT]))
                if g >= 2:
                    dve.wait_ge(tp_ready, KC * (g - 1))
                half, off = x_half[g // (GROUPS // 2)], (g % (GROUPS // 2)) * GT
                for t in range(GT):
                    tile = g * GT + t
                    last = dve.tensor_scalar(xn[:, g % 2, t, :], half[:, off + t, :], mean[:, tile:tile + 1],
                                             rstd[:, tile:tile + 1], ALU.subtract, ALU.mult)
                last.then_inc(xn_ready, 1)

            def keep_h(g):
                dve.wait_ge(h_ready, g + 1)
                dve.tensor_tensor(h_raw[:, g * GT:(g + 1) * GT, :], ps[:, H0:H0 + GT, 0:HW],
                                  b1x[:, :].unsqueeze(1).broadcast_to([P, GT, HW]), ALU.add).then_inc(h_kept, 1)

            def weights():
                dve.wait_ge(w_in, 16)
                dve.wait_ge(vec_in, 64)
                dve.memset(b1x[:, F:HW], 0.0)
                for kc in range(KC):
                    for a, dst in ((0, w1a1[:, kc:kc + 1]), (1, W1x[:, kc, F:F + 1])):
                        last = dve.tensor_tensor_reduce(out=junk[:, 2 * kc + a, :], in0=W1x[:, kc, 0:F], in1=ab[:, a, :],
                                                        scale=1.0, scalar=0.0, op0=ALU.mult, op1=ALU.add, accum_out=dst)
                link(last)
                for kc in range(KC):
                    last = dve.tensor_scalar(W1x[:, kc, F + 1:HW], w1a1[:, kc:kc + 1], 1 - SLOPE, None, ALU.mult)
                last.then_inc(const_ready, 1)

            def scalars():
                for a in range(2):
                    last = dve.tensor_tensor_reduce(out=junk[:, 4 + a, :], in0=b1x[:, 0:F], in1=ab[:, a, :], scale=1.0,
                                                    scalar=0.0, op0=ALU.mult, op1=ALU.add, accum_out=ba[:, a:a + 1])
                link(last)
                link(dve.tensor_tensor(gm[:, 6:7], ba[:, 0:1], ba[:, 1:2], ALU.add))
                link(dve.tensor_tensor(gm[:, 7:8], gm[:, 6:7], ba[:, 2:3], ALU.add))
                dve.memset(h_sum[:, F:F + 1], float(N))
                link(dve.memset(h_sum[:, F + 1:HW], 0.0))
                dve.wait_ge(pool_c, 3)
                dve.tensor_scalar(ones64[:, :], ones[:, :], 1.0 / 64, None, ALU.mult)

            moments(0)
            moments(1)
            normalise(0)
            weights()
            normalise(1)
            moments(2)
            for g in range(GROUPS):
                if g + 3 < GROUPS:
                    moments(g + 3)
                if g + 2 < GROUPS:
                    normalise(g + 2)
                if g == 2:
                    scalars()
                keep_h(g)

            dve.wait_ge(h_kept, GROUPS)
            dve.reduce_max(gm[:, 0:1], h_raw[:, :, F], AX.X).then_inc(pmax_ready, 1)
            dve.wait_ge(hn_ready, GROUPS * KC)
            link(dve.reduce_sum(hsum[:, :], hs[:, :, :], AX.X))
            for kc in range(KC):
                last = dve.tensor_scalar(hsrep[:, kc, :], ones[:, :], hsum[:, kc:kc + 1], None, ALU.mult)
            last.then_inc(hsrep_ready, 1)
            dve.wait_ge(pmaxT_ready, 1)
            dve.reduce_max(gm[0:1, 1:2], ps[0:1, 1, 0:P], AX.X).then_inc(g1_ready, 1)
            dve.wait_ge(g_ps, 1)
            link(dve.tensor_copy(gm[:, 2:3], ps[:, H0, 0:1]))
            dve.tensor_scalar(gm[:, 4:5], gm[:, 2:3], -(1 - SLOPE), None, ALU.mult)
            dve.tensor_scalar(gm[:, 5:6], gm[:, 2:3], -SLOPE, None, ALU.mult)
            last = dve.tensor_scalar(gm[:, 3:4], gm[:, 2:3], gm[:, 7:8], 1 - SLOPE, ALU.add, ALU.mult)
            last.then_inc(g_ready, 1)
            dve.wait_ge(g_ready, 1)
            dve.tensor_scalar(d8[:, :], h_raw[:, :, F], 1 - SLOPE, gm[:, 4:5], ALU.mult, ALU.add).then_inc(d8_ready, 1)

            def finish_S(ic):
                part = S[:, ds(ic * CW, CW)]
                dve.tensor_scalar(part, part, gm[:, 3:4], TOP, ALU.add, ALU.min).then_inc(S_ready, 1)

            dve.wait_ge(s_kept, GROUPS)
            finish_S(0)
            dve.wait_ge(qv_ready, 2)
            dve.wait_ge(d8_ready, 1)
            dve.memset(h_raw[:, :, F], 1.0)
            dve.memset(h_raw[:, :, F + 1], 0.0).then_inc(ones_col, 1)
            dve.wait_ge(hsum_ps, 1)
            link(dve.scalar_tensor_tensor(h_sum[:, 0:F], b1x[:, 0:F], float(N), ps[:, 0, 0:F], ALU.mult, ALU.add))
            link(dve.tensor_scalar(h_tiny[:, :], h_sum[:, :], TINY, None, ALU.mult))
            rest = slice(P // 2, P)
            dve.scalar_tensor_tensor(h_tiny[rest, :], h_sum[rest, :], TINY, h_tiny[rest, :].bitcast(fp32),
                                     ALU.mult, ALU.subtract).then_inc(prep_done, 1)

            def hp_low(r, c):
                for s in range(2):
                    jb = source(r, c) + s
                    dve.wait_ge(hp_tile, jb + 1)
                    dve.scalar_tensor_tensor(hp_lo[:, ds(jb, 1), :], h_raw[:, ds(jb, 1), :], v[:, ds(jb, 1)],
                                             hp_hi[:, ds(jb, 1), :].bitcast(fp32), ALU.mult, ALU.subtract)\
                        .then_inc(hp_ready, 1)

            def t_first(ic, r, c):
                if c in BOTH:
                    return
                n = pair_no(ic, r, c)
                if at_least(n, 2):
                    dve.wait_ge(masked, n - 1)
                dve.tensor_scalar(t_s[:, c % 2, 0, :], R[:, ds(ic * CW, CW)], q[:, ds(source(r, c), 1)], 1.0,
                                  ALU.mult, ALU.max).then_inc(dve_t, 1)

            def mask(ic, r, c):
                n = pair_no(ic, r, c)
                dve.wait_ge(adj_in[c], (ic * ROUNDS + r + 1) * 16)
                if c not in BOTH:
                    dve.wait_ge(dve_t, vector_t(ic, r, c))
                dve.wait_ge(act_t, n + 1)
                dve.scalar_tensor_tensor(adj_w[:, c, :, :], adj_s[:, c, :, :], 0.0, t_s[:, c % 2, :, :],
                                         ALU.is_gt, ALU.mult).then_inc(masked, 1)

            def low(ic, r, c):
                n = pair_no(ic, r, c)
                dve.wait_ge(hi_ready, n + 1)
                if at_least(n, 2):
                    dve.wait_ge(pe_done, n - 1)
                dve.tensor_tensor(w_lo[:, c % 2, :, :], adj_w[:, c, :, :], w_hi[:, c % 2, :, :].bitcast(fp32),
                                  ALU.subtract).then_inc(lo_ready, 1)

            def invert_y(ic):
                dve.wait_ge(evacuated, ic * BANKS + BANKS)
                dve.reciprocal(rden[:, :], y[:, :, F]).then_inc(y_ready, 1)

            def output(ic, hf):
                k = ic * 2 + hf
                dve.wait_ge(e_ready, (k + 1) * HALF)
                dve.tensor_scalar(e_s[:, :, :], e_s[:, :, :], 1.0, -1.0, ALU.min, ALU.add).then_inc(dve_y, 1)
                dve.wait_ge(dve_y, k + 1)
                for j in range(HALF):
                    ib = hf * HALF + j
                    last = dve.scalar_tensor_tensor(e_s[:, j, :].unsqueeze(1), y[:, ds(ib, 1), 0:F], rden[:, ds(ib, 1)],
                                                    e_s[:, j, :].unsqueeze(1), ALU.mult, ALU.max)
                last.then_inc(dve_o, 1)
                dve.wait_ge(xo_in, ic * 16 + 16)
                dve.wait_ge(dve_o, k + 1)
                o = o_s[:, ds(hf * HALF, HALF), :]
                dve.tensor_tensor(o, e_s[:, :, :], o, ALU.add).then_inc(summed, 1)

            def round_of(ic, r, first, last):
                inner = r is not FIRST_ROUND and r is not LAST_ROUND
                for c in range(SLOTS):
                    end = last and r is LAST_ROUND
                    if first and not (r is LAST_ROUND and c == SLOTS - 1):
                        hp_low(*ahead(ic, r, c, 1)[1:])
                    if not (end and c == SLOTS - 1):
                        mask(*ahead(ic, r, c, 1))
                    if not (end and c >= SLOTS - 2):
                        t_first(*ahead(ic, r, c, 2))
                    low(ic, r, c)
                    if r is FIRST_ROUND and c == 1 and not last:
                        finish_S(ic + 1)
                    if r is FIRST_ROUND and c == 3 and not first:
                        invert_y(ic - 1)
                    if inner and c == 3 and not first:
                        output(ic - 1, r - 1)
                    if r is LAST_ROUND and c == 0 and not last:
                        dve.wait_ge(R_ready, ic + 2)

            def chunk(ic, first=False, last=False):
                round_of(ic, FIRST_ROUND, first, last)
                with dve.Fori(1, ROUNDS - 1) as r:
                    round_of(ic, r, first, last)
                round_of(ic, LAST_ROUND, first, last)

            dve.wait_ge(R_ready, 1)
            t_first(0, 0, 0)
            t_first(0, 0, 1)
            hp_low(0, 0)
            mask(0, 0, 0)
            chunk(0, first=True)
            with dve.Fori(1, CHUNKS - 1) as ic:
                chunk(ic)
            chunk(CHUNKS - 1, last=True)
            def begin_end(ib):
                if ib < BANKS - 1:
                    dve.wait_ge(bank_done, (CHUNKS - 1) * (BANKS - 1) + ib + 1)
                else:
                    dve.wait_ge(pe_done, CHUNKS * PAIRS)
                dve.reciprocal(rden[:, ib:ib + 1], ps[:, ib, F:F + 1]).then_inc(rd_end, 1)

            dve.wait_ge(x_end_in, 16)
            begin_end(0)
            for ib in range(BANKS):
                if ib + 1 < BANKS:
                    begin_end(ib + 1)
                e, o = e_end[:, ib, :], x_end[:, ib, :]
                dve.wait_ge(e_end_ready, ib + 1)
                dve.tensor_scalar(e, e, 1.0, -1.0, ALU.min, ALU.add).then_inc(em_end, 1)
                dve.wait_ge(em_end, ib + 1)
                dve.scalar_tensor_tensor(e, ps[:, ib, 0:F], rden[:, ib:ib + 1], e, ALU.mult, ALU.max).then_inc(elu_end, 1)
                dve.wait_ge(elu_end, ib + 1)
                dve.tensor_tensor(o, e, o, ALU.add).then_inc(o_end, 1)


def kernel(x, adj, L0_gnn_W1, L0_gnn_b1, L0_gnn_a1, L0_gnn_a2, L0_gnn_b2):
    import numpy as np
    import concourse.bacc as bacc
    from concourse.bass_utils import run_bass_kernel_spmd

    tiles = np.asarray(adj).reshape(CHUNKS, CW, PAIRS, 2, P).transpose(0, 2, 4, 3, 1)
    arrays = {
        "adj_t": np.ascontiguousarray(tiles.reshape(CHUNKS * PAIRS, P, 2, CW)),
        "x": np.ascontiguousarray(x),
        "W1": np.ascontiguousarray(L0_gnn_W1),
        "b1": np.ascontiguousarray(L0_gnn_b1),
        "a1": np.ascontiguousarray(L0_gnn_a1),
        "a2": np.ascontiguousarray(L0_gnn_a2),
        "b2": np.ascontiguousarray(L0_gnn_b2).reshape(1),
    }
    nc = bacc.Bacc("TRN2", target_bir_lowering=False, num_devices=1)
    args = [nc.dram_tensor(name, a.shape, mybir.dt.from_np(a.dtype), kind="ExternalInput").ap()
            for name, a in arrays.items()]
    out = nc.dram_tensor("out", (N, F), mybir.dt.float32, kind="ExternalOutput").ap()
    build(nc, *args, out)
    r = run_bass_kernel_spmd(nc, [arrays], core_ids=[0])
    return r.results[0]["out"]
```

```python
from contextlib import ExitStack

import concourse.bass as bass
from concourse import mybir

P = 128
N = 4096
F = 256
KC = F // P
TILES = N // P
BANKS = 8
CW = BANKS * P
CHUNKS = N // CW
PAIRS = TILES // 2
SLOTS = 4
ROUNDS = PAIRS // SLOTS
GT = 4
GROUPS = TILES // GT
NORM_ACT = 2
HW = F + 2
EPS = 1e-5
SLOPE = 0.2
TOP = 70.0
HALF = 4
TINY = 2.0 ** -100
EARLY = 6 * GT
FIRST_ROUND, LAST_ROUND = 0, ROUNDS - 1


def pair_no(ic, r, c):
    return ic * PAIRS + r * SLOTS + c


def source(r, c):
    return r * (2 * SLOTS) + 2 * c


def ahead(ic, r, c, k):
    if c + k < SLOTS:
        return ic, r, c + k
    if r is LAST_ROUND:
        return ic + 1, 0, c + k - SLOTS
    return ic, r + 1, c + k - SLOTS


def at_least(n, least):
    return not isinstance(n, int) or n >= least


def build(nc, adj_t, x, W1, vectors, out):
    fp32, fp32r, i32 = mybir.dt.float32, mybir.dt.float32r, mybir.dt.int32
    ALU, ACT, AX = mybir.AluOpType, mybir.ActivationFunctionType, mybir.AxisListType
    ds = bass.ds

    x_v = x.rearrange("(t p) f -> p t f", p=P)
    out_v = out.rearrange("(t p) f -> p t f", p=P)

    ctx = ExitStack()
    with ctx:
        def sb(name, shape, dt=fp32):
            return ctx.enter_context(nc.sbuf_tensor(name, shape, dt))

        def over(name, shape, dt, host, skip=0):
            return nc.alloc_sbuf_tensor_at(name, shape, dt, offset=nc.lookup_mloc(host).addr + skip)

        def sem(name):
            return ctx.enter_context(nc.semaphore(name))

        hp_hi = sb("hp_hi", [P, TILES, HW], fp32r)
        hp_lo = sb("hp_lo", [P, TILES, HW], fp32r)
        h_raw = over("h_raw", [P, TILES, HW], fp32, hp_lo)
        R = sb("R", [P, N])
        adj_s = sb("adj_s", [P, SLOTS, 2, CW], i32)
        adj_w = adj_s[:, :, :, :].bitcast(fp32)
        w_hi = sb("w_hi", [P, SLOTS, 2, CW], fp32r)
        w_lo = sb("w_lo", [P, SLOTS, 2, CW], fp32r)
        y = sb("y", [P, BANKS, HW])
        e_s = sb("e_s", [P, HALF, F])
        o_s = sb("o_s", [P, BANKS, F])
        x_s = over("x_s", [P, TILES, F], fp32, w_lo)
        xn = over("xn", [P, 2, GT, F], fp32, w_hi, 2 * 2 * CW * 4)
        hnT = over("hnT", [P, 2, KC, GT * P], fp32r, w_hi, 3 * 2 * CW * 4)
        hnT_lo = over("hnT_lo", [P, 2, KC, GT * P], fp32r, w_hi, 2 * CW * 4)
        junk = over("junk", [P, 6, F], fp32, y)
        s1rep = over("s1rep", [P, 2, GT, P], fp32, e_s)
        hsrep = over("hsrep", [P, KC, P], fp32, o_s)
        vec = over("vec", [P, 3 * F + 1], fp32, o_s, KC * P * 4)
        W_lo = over("W_lo", [P, KC, HW], fp32r, o_s, KC * P * 4 + (3 * F + 8) * 4)
        W1x = over("W1x", [P, KC, HW], fp32, y, 6 * F * 4)
        x_end = adj_w[:, 0, :, :].rearrange("p s (b f) -> p (s b) f", f=F)
        e_end = y

        W_hi = sb("W_hi", [P, KC, HW], fp32r)
        b1x = sb("b1x", [P, HW])
        w1a1 = sb("w1a1", [P, KC])
        ident = sb("ident", [P, P])
        ones = sb("ones", [P, P])
        stats = sb("stats", [P, GROUPS, GT, 6])
        mom = sb("mom", [P, GROUPS, 4, GT])
        mean = sb("mean", [P, TILES])
        var = sb("var", [P, TILES])
        std = sb("std", [P, TILES])
        rstd = sb("rstd", [P, TILES])
        shift = sb("shift", [P, TILES])
        eps = sb("eps", [P, 1])
        ba = sb("ba", [P, 2])
        hs = sb("hs", [P, KC, GROUPS])
        hsum = sb("hsum", [P, KC])
        h_sum = sb("h_sum", [P, HW])
        h_tiny = sb("h_tiny", [P, HW], fp32r)
        ones64 = sb("ones64", [P, P], fp32r)
        gm = sb("gm", [P, 8])
        p = sb("p", [P, TILES])
        u = sb("u", [P, TILES])
        s2 = sb("s2", [P, TILES])
        cr = sb("cr", [P, TILES])
        cp = sb("cp", [P, TILES])
        rden = sb("rden", [P, BANKS])

        ps = ctx.enter_context(nc.psum_tensor("ps", [P, BANKS, 512], fp32))
        H0, S0 = 2, 6

        x_in = [sem(f"x_in{g}") for g in range(GROUPS)]
        w_in = sem("w_in")
        vec_in = sem("vec_in")
        adj_in = [sem(f"adj_in{s}") for s in range(SLOTS)]
        pool_c = sem("pool_c")
        pool_l = sem("pool_l")
        stat_ready = sem("stat_ready")
        rstd_ready = sem("rstd_ready")
        w1x_ready = sem("w1x_ready")
        g3_ready = sem("g3_ready")
        dve_c = sem("dve_c")
        const_ready = sem("const_ready")
        s1_ready = sem("s1_ready")
        var_ready = sem("var_ready")
        std_ready = sem("std_ready")
        xn_act = sem("xn_act")
        xn_ready = sem("xn_ready")
        tp_ready = sem("tp_ready")
        hn_ready = sem("hn_ready")
        hn_lo_ready = sem("hn_lo_ready")
        h_ready = sem("h_ready")
        h_kept = sem("h_kept")
        s_ready = sem("s_ready")
        s_kept = sem("s_kept")
        hsrep_ready = sem("hsrep_ready")
        hsum_ps = sem("hsum_ps")
        pmax_ready = sem("pmax_ready")
        pmaxT_ready = sem("pmaxT_ready")
        g1_ready = sem("g1_ready")
        g_ps = sem("g_ps")
        g_ready = sem("g_ready")
        c_ready = sem("c_ready")
        p_ready = sem("p_ready")
        u_ready = sem("u_ready")
        R_ready = sem("R_ready")
        ones_col = sem("ones_col")
        tiny_ready = sem("tiny_ready")
        prep_done = sem("prep_done")
        eps_ready = sem("eps_ready")
        hp_tile = sem("hp_tile")
        dve_y = sem("dve_y")
        dve_o = sem("dve_o")
        hp_first = sem("hp_first")
        hp_whole = sem("hp_whole")
        hp_ready = sem("hp_ready")
        signed = sem("signed")
        masked = sem("masked")
        hi_ready = sem("hi_ready")
        lo_ready = sem("lo_ready")
        pe_done = sem("pe_done")
        bank_done = sem("bank_done")
        evacuated = sem("evacuated")
        y_ready = sem("y_ready")
        e_ready = sem("e_ready")
        xo_in = sem("xo_in")
        x_end_in = sem("x_end_in")
        summed = sem("summed")
        rd_end = sem("rd_end")
        e_end_ready = sem("e_end_ready")
        em_end = sem("em_end")
        elu_end = sem("elu_end")
        o_end = sem("o_end")
        stored = sem("stored")
        stored_end = sem("stored_end")

        block = ctx.enter_context(nc.Block())

        @block.sync
        def _(sp):
            def load_nodes(g):
                sp.dma_start(x_s[:, g * GT:(g + 1) * GT, :], x_v[:, g * GT:(g + 1) * GT, :]).then_inc(x_in[g], 16)

            def load_adj(n, s):
                sp.dma_start(adj_s[:, s, :, :], adj_t[ds(n, 1), :, :, :].rearrange("a p s c -> p (a s) c"))\
                    .then_inc(adj_in[s], 16)

            def load_x(ic):
                sp.dma_start(o_s[:, :, :], x_v[:, ds(ic * BANKS, BANKS), :]).then_inc(xo_in, 16)

            def store(ic, hf):
                sp.wait_ge(summed, ic * 2 + hf + 2)
                sp.dma_start(out_v[:, ds(ic * BANKS + hf * HALF, HALF), :], o_s[:, hf * HALF:(hf + 1) * HALF, :])\
                    .then_inc(stored, 16)

            for g in range(GROUPS):
                load_nodes(g)
                if g == 3:
                    load_adj(0, 0)
            for s in range(1, SLOTS):
                load_adj(s, s)

            def chunk(ic, first=False, last=False):
                for r in range(ROUNDS):
                    for s in range(SLOTS):
                        n = pair_no(ic, r, s)
                        if not (last and r == LAST_ROUND):
                            sp.wait_ge(lo_ready, n + 1)
                            load_adj(n + SLOTS, s)
                        if not first and r in (2, 3) and s == 0:
                            store(ic - 1, r - 2)
                        if not last and (r, s) == (3, 3):
                            if not first:
                                sp.wait_ge(stored, ic * 32)
                            load_x(ic)
                        if last and (r, s) == (3, 0):
                            sp.wait_ge(lo_ready, n + 1)
                            sp.dma_start(x_end, x_v[:, (CHUNKS - 1) * BANKS:CHUNKS * BANKS, :]).then_inc(x_end_in, 16)

            chunk(0, first=True)
            with sp.Fori(1, CHUNKS - 1) as ic:
                chunk(ic)
            chunk(CHUNKS - 1, last=True)
            for ib in range(BANKS):
                sp.wait_ge(o_end, ib + 1)
                sp.dma_start(out_v[:, (CHUNKS - 1) * BANKS + ib, :], x_end[:, ib, :]).then_inc(stored_end, 16)
            sp.wait_ge(stored, (CHUNKS - 1) * 32)
            sp.wait_ge(stored_end, BANKS * 16)

        @block.gpsimd
        def _(pool):
            pool.memset(ones[:, :], 1.0).then_inc(pool_c, 1)
            pool.memset(ident[:, :], 0.0).then_inc(pool_c, 1)
            pool.wait_ge(pool_c, 2)
            pool.affine_select(out=ident[:, :], in_=ident[:, :], compare_op=ALU.not_equal, fill=1.0, base=0,
                               pattern=[[-1, P]], channel_multiplier=1).then_inc(pool_c, 1)
            links = [0]

            def link(ins):
                links[0] += 1
                ins.then_inc(pool_l, 1)
                pool.wait_ge(pool_l, links[0])

            def moments(g):
                pool.wait_ge(stat_ready, g + 1)
                st, mo = stats[:, g, :, :], mom[:, g, :, :]
                pool.tensor_tensor(mo[:, 0, :], st[:, :, 1], st[:, :, 4], ALU.add)
                pool.tensor_tensor(mo[:, 1, :], st[:, :, 1], st[:, :, 4], ALU.subtract)
                link(pool.tensor_tensor(mo[:, 2, :], st[:, :, 2], st[:, :, 5], ALU.add))
                pool.tensor_scalar(mean[:, g * GT:(g + 1) * GT], mo[:, 0, :], 0.5, None, ALU.mult)
                pool.tensor_tensor(mo[:, 3, :], mo[:, 1, :], mo[:, 1, :], ALU.mult)
                link(pool.tensor_scalar(mo[:, 2, :], mo[:, 2, :], 4.0 / F, None, ALU.mult))
                pool.tensor_tensor(var[:, g * GT:(g + 1) * GT], mo[:, 3, :], mo[:, 2, :], ALU.add).then_inc(var_ready, 1)

            def exponents(g):
                tiles = slice(g * GT, (g + 1) * GT)
                pool.wait_ge(h_kept, 2 * (g + 1))
                pool.tensor_scalar(cr[:, tiles], h_raw[:, tiles, F + 1], gm[:, 3:4], TOP, ALU.add, ALU.min)
                pool.tensor_copy(s2[:, tiles], h_raw[:, tiles, F])
                pool.tensor_scalar(cp[:, tiles], h_raw[:, tiles, F], -(1 - SLOPE), TOP, ALU.mult, ALU.min).then_inc(c_ready, 1)

            for g in range(4):
                moments(g)
            pool.wait_ge(g3_ready, 1)
            for g in range(GROUPS):
                if g + 4 < GROUPS:
                    moments(g + 4)
                exponents(g)

            def hp_low(jb):
                rows = h_raw[:, ds(jb, 1), :]
                pool.wait_ge(hp_tile, jb + 1)
                pool.tensor_tensor(rows, rows, u[:, ds(jb, 1)].unsqueeze(2).broadcast_to([P, 1, HW]), ALU.mult)\
                    .then_inc(hp_whole, 1)
                pool.wait_ge(hp_whole, jb - 1)
                pool.tensor_tensor(hp_lo[:, ds(jb, 1), :], rows, hp_hi[:, ds(jb, 1), :].bitcast(fp32), ALU.subtract)\
                    .then_inc(hp_ready, 1)

            with pool.Fori(2, TILES) as jb:
                hp_low(jb)

            pool.wait_ge(x_end_in, 16)
            for ib in range(BANKS):
                o = x_end[:, ib, :]
                pool.wait_ge(elu_end, ib + 1)
                pool.tensor_tensor(o, e_end[:, ib, 0:F], o, ALU.add).then_inc(o_end, 1)

        @block.scalar
        def _(act):
            act.dma_start(W1x[:, :, 0:F], W1.rearrange("(c p) f -> p c f", p=P)).then_inc(w_in, 16)
            act.dma_start(vec[:, :], vectors.partition_broadcast(P)).then_inc(vec_in, 16)

            def root(g):
                act.wait_ge(var_ready, g + 1)
                act.activation(std[:, g * GT:(g + 1) * GT], var[:, g * GT:(g + 1) * GT], ACT.Sqrt,
                               scale=1.0 / 4, bias=eps[:, 0:1]).then_inc(std_ready, 1)

            def normalise(g):
                act.wait_ge(rstd_ready, g + 1)
                if g >= 2:
                    act.wait_ge(tp_ready, KC * (g - 1))
                for t in range(NORM_ACT):
                    tile = g * GT + t
                    last = act.activation(xn[:, g % 2, t, :], x_s[:, tile, :], ACT.Identity,
                                          scale=rstd[:, tile:tile + 1], bias=shift[:, tile:tile + 1])
                last.then_inc(xn_act, 1)

            def relu_T(g):
                if g >= 2:
                    act.wait_ge(h_ready, 2 * (g - 1))
                for kc in range(KC):
                    act.wait_ge(tp_ready, KC * g + kc + 1)
                    act.activation(hnT[:, g % 2, kc, :], ps[:, kc, :], ACT.Relu,
                                   accum_out=hs[:, kc, g:g + 1]).then_inc(hn_ready, 1)

            def repeat_s1(g):
                if g >= 2:
                    act.wait_ge(s_ready, g - 1)
                act.wait_ge(c_ready, g + 1)
                act.activation(s1rep[:, g % 2, :, :],
                               cr[:, g * GT:(g + 1) * GT].unsqueeze(2).broadcast_to([P, GT, P]),
                               ACT.Copy).then_inc(s1_ready, 1)

            def keep_s(g):
                act.wait_ge(s_ready, g + 1)
                act.activation(R[:, g * GT * P:(g + 1) * GT * P], ps[:, S0 + g % 2, :], ACT.Copy).then_inc(s_kept, 1)

            def exp_R(ic):
                part = R[:, ds(ic * CW, CW)]
                act.activation(part, part, ACT.Exp).then_inc(R_ready, 1)

            def sign(ic, r, c):
                act.wait_ge(adj_in[c], (ic * ROUNDS + r + 1) * 16)
                act.activation(adj_w[:, c, :, :], adj_s[:, c, :, :], ACT.Sign).then_inc(signed, 1)

            def high(ic, r, c):
                n = pair_no(ic, r, c)
                act.wait_ge(masked, n + 1)
                if at_least(n, SLOTS):
                    act.wait_ge(pe_done, n - SLOTS + 1)
                act.activation(w_hi[:, c, :, :], adj_w[:, c, :, :], ACT.Relu).then_inc(hi_ready, 1)

            act.preload_act_table(ACT.Sqrt)
            act.wait_ge(eps_ready, 1)
            root(0)
            normalise(0)
            root(1)
            normalise(1)
            relu_T(0)
            sign(0, 0, 0)
            for g in range(GROUPS):
                if g + 1 < GROUPS:
                    relu_T(g + 1)
                if g == 0:
                    root(2)
                if g + 2 < GROUPS:
                    normalise(g + 2)
                if g + 3 < GROUPS:
                    root(g + 3)
                if g >= 1:
                    repeat_s1(g - 1)
                if g == 6:
                    act.wait_ge(c_ready, EARLY // GT)
                    act.activation(p[:, 0:EARLY], cp[:, 0:EARLY], ACT.Exp).then_inc(p_ready, 1)
                    act.wait_ge(s_kept, CW // (GT * P))
                    exp_R(0)
                if g >= 2:
                    keep_s(g - 2)
                if g == 7:
                    high(0, 0, 0)
                if g == 2:
                    sign(0, 0, 1)
            repeat_s1(GROUPS - 1)
            act.activation(p[:, EARLY:TILES], cp[:, EARLY:TILES], ACT.Exp).then_inc(p_ready, 1)

            act.wait_ge(g_ready, 1)
            act.activation(u[:, :], s2[:, :], ACT.Exp, bias=gm[:, 4:5]).then_inc(u_ready, 1)

            def hp_high(r, c):
                for s in range(2):
                    jb = source(r, c) + s
                    act.activation(hp_hi[:, ds(jb, 1), :], h_raw[:, ds(jb, 1), :], ACT.Copy,
                                   scale=u[:, ds(jb, 1)]).then_inc(hp_tile, 1)

            def evacuate(ic):
                act.wait_ge(summed, 2 * ic + 1)
                for ib in range(BANKS):
                    if ib < BANKS - 1:
                        act.wait_ge(bank_done, ic * (BANKS - 1) + ib + 1)
                    else:
                        act.wait_ge(pe_done, ic * PAIRS + PAIRS)
                    act.activation(y[:, ib, :], ps[:, ib, 0:HW], ACT.Copy).then_inc(evacuated, 1)

            def exp_y(ic, hf, js):
                for j in js:
                    ib = hf * HALF + j
                    act.activation(e_s[:, j, :].unsqueeze(1), y[:, ds(ib, 1), 0:F], ACT.Exp,
                                   scale=rden[:, ds(ib, 1)]).then_inc(e_ready, 1)

            def round_of(ic, r, first, last):
                inner = r is not FIRST_ROUND and r is not LAST_ROUND
                for c in range(SLOTS):
                    if first and not (r is LAST_ROUND and c == SLOTS - 1):
                        hp_high(*ahead(ic, r, c, 1)[1:])
                    if inner and c == 1 and not first:
                        act.wait_ge(y_ready, ic)
                        act.wait_ge(summed, (ic - 1) * 2 + r)
                    if not (first and r is FIRST_ROUND and c == 0):
                        high(ic, r, c)
                    if r is FIRST_ROUND and c == 0 and not first:
                        evacuate(ic - 1)
                    if not (last and r is LAST_ROUND and c >= SLOTS - 2):
                        sign(*ahead(ic, r, c, 2))
                    if r is FIRST_ROUND and c == 2 and not last:
                        exp_R(ic + 1)
                    if inner and not first and c in (1, 2):
                        exp_y(ic - 1, r - 1, (2 * c - 2, 2 * c - 1))

            def chunk(ic, first=False, last=False):
                round_of(ic, FIRST_ROUND, first, last)
                with act.Fori(1, ROUNDS - 1) as r:
                    round_of(ic, r, first, last)
                round_of(ic, LAST_ROUND, first, last)

            act.wait_ge(ones_col, 1)
            act.wait_ge(u_ready, 1)
            hp_high(0, 0)
            keep_s(GROUPS - 2)
            keep_s(GROUPS - 1)
            act.wait_ge(s_kept, GROUPS)
            chunk(0, first=True)
            with act.Fori(1, CHUNKS - 1) as ic:
                chunk(ic)
            chunk(CHUNKS - 1, last=True)
            for ib in range(BANKS):
                act.wait_ge(rd_end, ib + 1)
                act.activation(e_end[:, ib, 0:F], ps[:, ib, 0:F], ACT.Exp, scale=rden[:, ib:ib + 1]).then_inc(e_end_ready, 1)

        @block.tensor
        def _(pe):
            def transposes(g, u):
                pe.wait_ge(xn_ready, g + 1)
                pe.wait_ge(xn_act, g + 1)
                for kc in range(KC):
                    if at_least(g, 1):
                        pe.wait_ge(hn_lo_ready, (g - 1) * KC + kc + 1)
                    for t in range(GT):
                        last = pe.transpose(ps[:, kc, t * P:(t + 1) * P], xn[:, u, t, kc * P:(kc + 1) * P],
                                            ident[:, :])
                    last.then_inc(tp_ready, 1)

            def project(g, u):
                pe.wait_ge(hn_lo_ready, g * KC + KC)
                for t in range(GT):
                    if at_least(g, 1) and t % (GT // 2) == 0:
                        pe.wait_ge(h_kept, 2 * g - 1 + t // (GT // 2))
                    acc, node = ps[:, H0 + t, 0:HW], slice(t * P, (t + 1) * P)
                    for kc in range(KC):
                        pe.matmul(acc, hnT[:, u, kc, node], W_hi[:, kc, :], start=kc == 0, stop=False)
                        pe.matmul(acc, hnT[:, u, kc, node], W_lo[:, kc, :], start=False, stop=False)
                        last = pe.matmul(acc, hnT_lo[:, u, kc, node], W_hi[:, kc, :], start=False, stop=kc == KC - 1)
                    if t % (GT // 2) == GT // 2 - 1:
                        last.then_inc(h_ready, 1)

            def spread(g, u):
                pe.wait_ge(s1_ready, g + 1)
                if at_least(g, 2):
                    pe.wait_ge(s_kept, g - 1)
                for t in range(GT):
                    last = pe.transpose(ps[:, S0 + u, t * P:(t + 1) * P], s1rep[:, u, t, :], ident[:, :])
                last.then_inc(s_ready, 1)

            pe.wait_ge(pool_c, 3)
            transposes(0, 0)
            pe.wait_ge(const_ready, 1)
            transposes(1, 1)
            project(0, 0)
            transposes(2, 0)
            project(1, 1)
            spread(0, 0)
            transposes(3, 1)
            project(2, 0)
            spread(1, 1)
            with pe.Fori(2, GROUPS // 2) as k:
                transposes(2 * k, 0)
                project(2 * k - 1, 1)
                spread(2 * k - 2, 0)
                transposes(2 * k + 1, 1)
                project(2 * k, 0)
                spread(2 * k - 1, 1)
            project(GROUPS - 1, 1)
            pe.wait_ge(hsrep_ready, 1)
            for kc in range(KC):
                last = pe.matmul(ps[:, 0, 0:F], hsrep[:, kc, :], W1x[:, kc, 0:F], start=kc == 0, stop=kc == KC - 1)
            last.then_inc(hsum_ps, 1)
            spread(GROUPS - 2, 0)
            pe.wait_ge(pmax_ready, 1)
            pe.transpose(ps[0:1, 1, 0:P], gm[:, 0:1], ident[:, :]).then_inc(pmaxT_ready, 1)
            pe.wait_ge(g1_ready, 1)
            pe.matmul(ps[:, H0, 0:1], ones[0:1, 0:P], gm[0:1, 1:2], start=True, stop=True).then_inc(g_ps, 1)
            spread(GROUPS - 1, 1)

            def start_sum(ib):
                pe.matmul(ps[:, ib, 0:HW], ones64[:, :], h_tiny[:, :], start=True, stop=False)

            def pair(ic, m, b, first, begin=False):
                n = ic * PAIRS + m
                for part, w in ((0, w_hi), (1, w_lo)):
                    pe.wait_ge((hi_ready, lo_ready)[part], n + 1)
                    for s in range(2):
                        if first and part == 0:
                            if begin:
                                pe.wait_ge(hp_first, s + 1)
                            else:
                                pe.wait_ge(hp_ready, 2 * m + s - 1)
                        hh = hp_hi[:, ds(2 * m + s, 1), :]
                        hl = hp_lo[:, ds(2 * m + s, 1), :]
                        for ib in range(BANKS):
                            acc = ps[:, ib, 0:HW].unsqueeze(1)
                            block_w = w[:, b, s, ib * P:(ib + 1) * P]
                            if begin and part == 0 and s == 0 and not (first and ib < S0):
                                if first:
                                    pe.wait_ge(s_kept, GROUPS + ib - S0 - 1)
                                else:
                                    pe.wait_ge(evacuated, (ic - 1) * BANKS + ib + 1)
                                start_sum(ib)
                            last = pe.matmul(acc, block_w, hh, start=False, stop=False)
                            if part == 0:
                                pe.matmul(acc, block_w, hl, start=False, stop=False)
                last.then_inc(pe_done, 1)

            def last_pair(ic, m, b, first):
                pe.wait_ge(lo_ready, ic * PAIRS + m + 1)
                if first:
                    pe.wait_ge(hp_ready, 2 * m)
                for ib in range(BANKS):
                    acc = ps[:, ib, 0:HW].unsqueeze(1)
                    col = slice(ib * P, (ib + 1) * P)
                    for s in range(2):
                        hh = hp_hi[:, ds(2 * m + s, 1), :]
                        hl = hp_lo[:, ds(2 * m + s, 1), :]
                        pe.matmul(acc, w_hi[:, b, s, col], hh, start=False, stop=False)
                        pe.matmul(acc, w_hi[:, b, s, col], hl, start=False, stop=False)
                        last = pe.matmul(acc, w_lo[:, b, s, col], hh, start=False, stop=s == 1)
                    if ib < BANKS - 1:
                        last.then_inc(bank_done, 1)
                last.then_inc(pe_done, 1)

            def chunk(ic, first=False):
                for b in range(SLOTS):
                    pair(ic, b, b, first, begin=b == 0)
                with pe.Fori(1, ROUNDS - 1) as r:
                    for b in range(SLOTS):
                        pair(ic, r * SLOTS + b, b, first)
                for b in range(SLOTS - 1):
                    pair(ic, PAIRS - SLOTS + b, b, first)
                last_pair(ic, PAIRS - 1, SLOTS - 1, first)

            pe.wait_ge(prep_done, 1)
            for ib in range(S0):
                start_sum(ib)
            chunk(0, first=True)
            with pe.Fori(1, CHUNKS) as ic:
                chunk(ic)

        @block.vector
        def _(dve):
            links = [0]

            def link(ins):
                links[0] += 1
                ins.then_inc(dve_c, 1)
                dve.wait_ge(dve_c, links[0])

            dve.sem_inc(summed, 1)
            dve.memset(eps[:, :], EPS).then_inc(eps_ready, 1)

            def statistics(g):
                dve.wait_ge(x_in[g], 16)
                for t in range(GT):
                    last = dve.bn_stats(stats[:, g, t, :], x_s[:, g * GT + t, :])
                last.then_inc(stat_ready, 1)

            def invert(g):
                tiles = slice(g * GT, (g + 1) * GT)
                dve.wait_ge(std_ready, g + 1)
                link(dve.reciprocal(rstd[:, tiles], std[:, tiles]))
                dve.scalar_tensor_tensor(shift[:, tiles], mean[:, tiles], -1.0, rstd[:, tiles], ALU.mult, ALU.mult)\
                    .then_inc(rstd_ready, 1)

            def normalise(g):
                if g >= 2:
                    dve.wait_ge(tp_ready, KC * (g - 1))
                for t in range(NORM_ACT, GT):
                    tile = g * GT + t
                    last = dve.tensor_scalar(xn[:, g % 2, t, :], x_s[:, tile, :], mean[:, tile:tile + 1],
                                             rstd[:, tile:tile + 1], ALU.subtract, ALU.mult)
                last.then_inc(xn_ready, 1)

            def low_T(g):
                if g >= 2:
                    dve.wait_ge(h_ready, 2 * (g - 1))
                for kc in range(KC):
                    dve.wait_ge(hn_ready, KC * g + kc + 1)
                    dve.scalar_tensor_tensor(hnT_lo[:, g % 2, kc, :], ps[:, kc, :], 0.0,
                                             hnT[:, g % 2, kc, :].bitcast(fp32), ALU.max, ALU.subtract)\
                        .then_inc(hn_lo_ready, 1)

            def keep_h(g):
                for hf in range(2):
                    dve.wait_ge(h_ready, 2 * g + hf + 1)
                    t0 = hf * GT // 2
                    dve.tensor_tensor(h_raw[:, g * GT + t0:g * GT + t0 + GT // 2, :], ps[:, H0 + t0:H0 + t0 + GT // 2, 0:HW],
                                      b1x[:, :].unsqueeze(1).broadcast_to([P, GT // 2, HW]), ALU.add).then_inc(h_kept, 1)

            def weights():
                dve.wait_ge(w_in, 16)
                dve.wait_ge(vec_in, 16)
                dve.tensor_copy(b1x[:, 0:F], vec[:, 2 * F:3 * F])
                dve.memset(b1x[:, F:HW], 0.0)
                for kc in range(KC):
                    for a, dst in ((0, w1a1[:, kc:kc + 1]), (1, W1x[:, kc, F:F + 1])):
                        last = dve.tensor_tensor_reduce(out=junk[:, 2 * kc + a, :], in0=W1x[:, kc, 0:F], in1=vec[:, a * F:(a + 1) * F],
                                                        scale=1.0, scalar=0.0, op0=ALU.mult, op1=ALU.add, accum_out=dst)
                link(last)
                for kc in range(KC):
                    last = dve.tensor_scalar(W1x[:, kc, F + 1:HW], w1a1[:, kc:kc + 1], 1 - SLOPE, None, ALU.mult)
                last.then_inc(w1x_ready, 1)

            def split_weights():
                dve.wait_ge(w1x_ready, 1)
                link(dve.tensor_copy(W_hi[:, :, :], W1x[:, :, :]))
                dve.tensor_tensor(W_lo[:, :, :], W1x[:, :, :], W_hi[:, :, :].bitcast(fp32), ALU.subtract).then_inc(const_ready, 1)

            def scalars():
                for a in range(2):
                    last = dve.tensor_tensor_reduce(out=junk[:, 4 + a, :], in0=vec[:, 2 * F:3 * F], in1=vec[:, a * F:(a + 1) * F], scale=1.0,
                                                    scalar=0.0, op0=ALU.mult, op1=ALU.add, accum_out=ba[:, a:a + 1])
                link(last)
                link(dve.tensor_tensor(gm[:, 6:7], ba[:, 0:1], ba[:, 1:2], ALU.add))
                dve.tensor_scalar(gm[:, 3:4], gm[:, 6:7], vec[:, 3 * F:3 * F + 1], 1 - SLOPE, ALU.add, ALU.mult).then_inc(g3_ready, 1)

            def mask(ic, r, c):
                n = pair_no(ic, r, c)
                dve.wait_ge(signed, n + 1)
                for s in range(2):
                    sgn = adj_w[:, c, s, :]
                    last = dve.scalar_tensor_tensor(sgn, R[:, ds(ic * CW, CW)], p[:, ds(source(r, c) + s, 1)], sgn,
                                                    ALU.max, ALU.mult)
                last.then_inc(masked, 1)

            def low(ic, r, c):
                n = pair_no(ic, r, c)
                dve.wait_ge(hi_ready, n + 1)
                if at_least(n, SLOTS):
                    dve.wait_ge(pe_done, n - SLOTS + 1)
                dve.scalar_tensor_tensor(w_lo[:, c, :, :], adj_w[:, c, :, :], 0.0, w_hi[:, c, :, :].bitcast(fp32),
                                         ALU.max, ALU.subtract).then_inc(lo_ready, 1)

            statistics(0)
            statistics(1)
            invert(0)
            normalise(0)
            weights()
            invert(1)
            normalise(1)
            split_weights()
            low_T(0)
            statistics(2)
            scalars()
            statistics(3)
            for g in range(GROUPS):
                if 0 < g < GROUPS - 2:
                    invert(g + 2)
                if g + 1 < GROUPS:
                    low_T(g + 1)
                if g == 0:
                    invert(2)
                if g + 2 < GROUPS:
                    normalise(g + 2)
                if g + 4 < GROUPS:
                    statistics(g + 4)
                if g == 4:
                    dve.wait_ge(pool_c, 3)
                    dve.memset(h_sum[:, F:F + 1], float(N))
                    link(dve.memset(h_sum[:, F + 1:HW], 0.0))
                    dve.tensor_scalar(ones64[:, :], ones[:, :], 1.0 / 64, None, ALU.mult)
                if g == 7:
                    dve.wait_ge(hn_ready, GROUPS * KC)
                    link(dve.reduce_sum(hsum[:, :], hs[:, :, :], AX.X))
                    for kc in range(KC):
                        last = dve.tensor_scalar(hsrep[:, kc, :], ones[:, :], hsum[:, kc:kc + 1], None, ALU.mult)
                    last.then_inc(hsrep_ready, 1)
                    dve.wait_ge(p_ready, 1)
                    dve.wait_ge(R_ready, 1)
                    mask(0, 0, 0)
                keep_h(g)

            dve.wait_ge(h_kept, 2 * GROUPS)
            dve.reduce_max(gm[:, 0:1], h_raw[:, :, F], AX.X).then_inc(pmax_ready, 1)
            dve.wait_ge(pmaxT_ready, 1)
            dve.reduce_max(gm[0:1, 1:2], ps[0:1, 1, 0:P], AX.X).then_inc(g1_ready, 1)
            dve.wait_ge(c_ready, GROUPS)
            dve.wait_ge(pmax_ready, 1)
            dve.memset(h_raw[:, :, F], 1.0)
            dve.memset(h_raw[:, :, F + 1], 0.0).then_inc(ones_col, 1)
            dve.wait_ge(hsum_ps, 1)
            link(dve.scalar_tensor_tensor(h_sum[:, 0:F], b1x[:, 0:F], float(N), ps[:, 0, 0:F], ALU.mult, ALU.add))
            dve.wait_ge(g_ps, 1)
            dve.tensor_scalar(gm[:, 4:5], ps[:, H0, 0:1], -1.0, None, ALU.mult).then_inc(g_ready, 1)
            dve.tensor_scalar(h_tiny[:, :], h_sum[:, :], TINY, None, ALU.mult).then_inc(tiny_ready, 1)
            rest = slice(P // 2, P)
            dve.wait_ge(tiny_ready, 1)
            dve.scalar_tensor_tensor(h_tiny[rest, :], h_sum[rest, :], TINY, h_tiny[rest, :].bitcast(fp32),
                                     ALU.mult, ALU.subtract).then_inc(prep_done, 1)

            def invert_y(ic):
                dve.wait_ge(evacuated, ic * BANKS + BANKS)
                dve.reciprocal(rden[:, :], y[:, :, F]).then_inc(y_ready, 1)

            def output(ic, hf):
                k = ic * 2 + hf
                dve.wait_ge(e_ready, (k + 1) * HALF)
                dve.tensor_scalar(e_s[:, :, :], e_s[:, :, :], 1.0, -1.0, ALU.min, ALU.add).then_inc(dve_y, 1)
                dve.wait_ge(dve_y, k + 1)
                for j in range(HALF):
                    ib = hf * HALF + j
                    last = dve.scalar_tensor_tensor(e_s[:, j, :].unsqueeze(1), y[:, ds(ib, 1), 0:F], rden[:, ds(ib, 1)],
                                                    e_s[:, j, :].unsqueeze(1), ALU.mult, ALU.max)
                last.then_inc(dve_o, 1)
                dve.wait_ge(xo_in, ic * 16 + 16)
                dve.wait_ge(dve_o, k + 1)
                o = o_s[:, ds(hf * HALF, HALF), :]
                dve.tensor_tensor(o, e_s[:, :, :], o, ALU.add).then_inc(summed, 1)

            def round_of(ic, r, first, last):
                inner = r is not FIRST_ROUND and r is not LAST_ROUND
                for c in range(SLOTS):
                    end = last and r is LAST_ROUND
                    if not (end and c == SLOTS - 1):
                        mask(*ahead(ic, r, c, 1))
                    low(ic, r, c)
                    if r is FIRST_ROUND and c == 3 and not first:
                        invert_y(ic - 1)
                    if inner and c == 3 and not first:
                        output(ic - 1, r - 1)
                    if r is LAST_ROUND and c == 0 and not last:
                        dve.wait_ge(R_ready, ic + 2)

            def chunk(ic, first=False, last=False):
                round_of(ic, FIRST_ROUND, first, last)
                with dve.Fori(1, ROUNDS - 1) as r:
                    round_of(ic, r, first, last)
                round_of(ic, LAST_ROUND, first, last)

            for jb in range(2):
                dve.wait_ge(hp_tile, jb + 1)
                dve.scalar_tensor_tensor(hp_lo[:, jb, :], h_raw[:, jb, :], u[:, jb:jb + 1], hp_hi[:, jb, :].bitcast(fp32),
                                         ALU.mult, ALU.subtract).then_inc(hp_first, 1)
            dve.wait_ge(p_ready, 2)
            chunk(0, first=True)
            with dve.Fori(1, CHUNKS - 1) as ic:
                chunk(ic)
            chunk(CHUNKS - 1, last=True)
            def begin_end(ib):
                if ib < BANKS - 1:
                    dve.wait_ge(bank_done, (CHUNKS - 1) * (BANKS - 1) + ib + 1)
                else:
                    dve.wait_ge(pe_done, CHUNKS * PAIRS)
                dve.reciprocal(rden[:, ib:ib + 1], ps[:, ib, F:F + 1]).then_inc(rd_end, 1)

            dve.wait_ge(summed, 2 * CHUNKS - 1)
            begin_end(0)
            for ib in range(BANKS):
                if ib + 1 < BANKS:
                    begin_end(ib + 1)
                e = e_end[:, ib, 0:F]
                dve.wait_ge(e_end_ready, ib + 1)
                dve.tensor_scalar(e, e, 1.0, -1.0, ALU.min, ALU.add).then_inc(em_end, 1)
                dve.wait_ge(em_end, ib + 1)
                dve.scalar_tensor_tensor(e, ps[:, ib, 0:F], rden[:, ib:ib + 1], e, ALU.mult, ALU.max).then_inc(elu_end, 1)


def kernel(x, adj, L0_gnn_W1, L0_gnn_b1, L0_gnn_a1, L0_gnn_a2, L0_gnn_b2):
    import numpy as np
    import concourse.bacc as bacc
    from concourse.bass_utils import run_bass_kernel_spmd

    tiles = np.asarray(adj).reshape(CHUNKS, CW, PAIRS, 2, P).transpose(0, 2, 4, 3, 1)
    arrays = {
        "adj_t": np.ascontiguousarray(tiles.reshape(CHUNKS * PAIRS, P, 2, CW)),
        "x": np.ascontiguousarray(x),
        "W1": np.ascontiguousarray(L0_gnn_W1),
        "vectors": np.concatenate([np.ravel(a) for a in (L0_gnn_a1, L0_gnn_a2, L0_gnn_b1, L0_gnn_b2)]),
    }
    nc = bacc.Bacc("TRN2", target_bir_lowering=False, num_devices=1)
    args = [nc.dram_tensor(name, a.shape, mybir.dt.from_np(a.dtype), kind="ExternalInput").ap()
            for name, a in arrays.items()]
    out = nc.dram_tensor("out", (N, F), mybir.dt.float32, kind="ExternalOutput").ap()
    build(nc, *args, out)
    r = run_bass_kernel_spmd(nc, [arrays], core_ids=[0])
    return r.results[0]["out"]
```
